# Optimizing a Trainium2 kernel written in Bass

```python
import numpy as np
import jax
import jax.numpy as jnp

def _softmax(x, axis=-1):
    return jax.nn.softmax(x, axis=axis)

def _gelu(x):
    return jax.nn.gelu(x, approximate=True)

def _silu(x):
    return jax.nn.silu(x)

def _sigmoid(x):
    return jax.nn.sigmoid(x)

def _layernorm(x, axis=-1, eps=1e-05):
    m = jnp.mean(x, axis=axis, keepdims=True)
    v = jnp.var(x, axis=axis, keepdims=True)
    return (x - m) / jnp.sqrt(v + eps)

def _scatter_add(tgt, idx, src, axis=0):
    return tgt.at[idx].add(src)

def _segment_sum(src, seg, n):
    return jax.ops.segment_sum(src, seg, n)
kernel_name = 'mk_seq_postln_d1_jaxref_r4_a902ff'

def setup_inputs(seed: int=0):
    np.random.seed(seed)
    _w = jnp.asarray

    def _L0_attn_setup():
        import jax, jax.numpy as jnp
        import numpy as np
        DIM = 256
        N_HEADS = 16
        HEAD_DIM = DIM // N_HEADS
        SCALE = HEAD_DIM ** (-0.5)
        key = jax.random.key(seed)
        k1, k2, k3 = jax.random.split(key, 3)
        x = jax.random.normal(k1, (4, 512, DIM), dtype=jnp.float32)
        w_qkv = jax.random.normal(k2, (DIM, 3 * DIM), dtype=jnp.float32) * DIM ** (-0.5)
        w_proj = jax.random.normal(k3, (DIM, DIM), dtype=jnp.float32) * DIM ** (-0.5)
        b_proj = jnp.zeros((DIM,), dtype=jnp.float32)
        return {'x': x, 'w_qkv': w_qkv, 'w_proj': w_proj, 'b_proj': b_proj}
    _L0_attn_in = _L0_attn_setup()

    def _L0_ffn_setup():
        import jax, jax.numpy as jnp
        import numpy as np
        B, C, D = (2, 512, 256)
        I = 512
        E, K = (8, 2)
        CF = 1.25
        key = jax.random.key(seed)
        k1, k2, k3, k4 = jax.random.split(key, 4)
        scale = 0.02
        return {'hidden_states': jax.random.normal(k1, (B, C, D), jnp.float32), 'Wg': jax.random.normal(k2, (E, D), jnp.float32) * scale, 'W1': jax.random.normal(k3, (E, D, 2 * I), jnp.float32) * scale, 'W2': jax.random.normal(k4, (E, I, D), jnp.float32) * scale}
    _L0_ffn_in = _L0_ffn_setup()
    _d = {'L0_attn_x': _L0_attn_in['x'], 'L0_attn_w_qkv': _L0_attn_in['w_qkv'], 'L0_attn_w_proj': _L0_attn_in['w_proj'], 'L0_attn_b_proj': _L0_attn_in['b_proj'], 'L0_ffn_Wg': _L0_ffn_in['Wg'], 'L0_ffn_W1': _L0_ffn_in['W1'], 'L0_ffn_W2': _L0_ffn_in['W2']}
    _x0 = _d['L0_attn_x']
    _d['L0_attn_x'] = jax.random.normal(jax.random.fold_in(jax.random.key(seed), 1), (32, 512, 256), dtype=_x0.dtype)
    del _x0
    return _d

def reference(L0_attn_x, L0_attn_w_qkv, L0_attn_w_proj, L0_attn_b_proj, L0_ffn_Wg, L0_ffn_W1, L0_ffn_W2):

    def _L0_attn_ref(x, w_qkv, w_proj, b_proj):
        import jax, jax.numpy as jnp
        import numpy as np
        DIM = 256
        N_HEADS = 16
        HEAD_DIM = DIM // N_HEADS
        SCALE = HEAD_DIM ** (-0.5)
        b, s, d = x.shape
        qkv = (x @ w_qkv).reshape(b, s, 3, N_HEADS, HEAD_DIM)
        q, k, v = jnp.moveaxis(qkv, 2, 0)
        scores = jnp.einsum('bqhd,bkhd->bhqk', q, k) * SCALE
        attn = jax.nn.softmax(scores, axis=-1)
        out = jnp.einsum('bhqk,bkhd->bqhd', attn, v).reshape(b, s, d)
        return out @ w_proj + b_proj

    def _L0_ffn_ref(hidden_states, Wg, W1, W2):
        import jax, jax.numpy as jnp
        import numpy as np
        B, C, D = (2, 512, 256)
        I = 512
        E, K = (8, 2)
        CF = 1.25
        Bx, Cx, d = hidden_states.shape
        N = Bx * Cx
        cap = int(N * K * CF / E)
        x = hidden_states.reshape(N, d)
        logits = x @ Wg.T
        top_v, top_i = jax.lax.top_k(logits, K)
        gates = jax.nn.softmax(top_v, axis=-1)
        flat_e = top_i.reshape(N * K)
        gates_f = gates.reshape(N * K)
        tok = jnp.repeat(jnp.arange(N), K)
        onehot = jax.nn.one_hot(flat_e, E, dtype=jnp.int32)
        pos = jnp.cumsum(onehot, axis=0) - 1
        pos_f = jnp.take_along_axis(pos, flat_e[:, None], axis=1)[:, 0]
        keep = pos_f < cap
        pos_safe = jnp.where(keep, pos_f, cap)
        exp_batches = jnp.zeros((E, cap, d), x.dtype).at[flat_e, pos_safe].set(x[tok], mode='drop')
        h = jnp.einsum('ecd,edf->ecf', exp_batches, W1)
        inp, gate = jnp.split(h, 2, axis=-1)
        h = jax.nn.gelu(inp, approximate=False) * gate
        exp_out = jnp.einsum('eci,eid->ecd', h, W2)
        gathered = exp_out[flat_e, jnp.minimum(pos_safe, cap - 1)]
        contrib = jnp.where(keep, gates_f, 0.0)[:, None] * gathered
        out = jax.ops.segment_sum(contrib, tok, num_segments=N)
        return out.reshape(Bx, Cx, d)
    x = L0_attn_x
    x = _layernorm(x + _L0_attn_ref(x, L0_attn_w_qkv, L0_attn_w_proj, L0_attn_b_proj), axis=-1)
    x = _layernorm(x + _L0_ffn_ref(x, L0_ffn_Wg, L0_ffn_W1, L0_ffn_W2), axis=-1)
    return x

_drawn_inputs = setup_inputs


def setup_inputs(seed=0):
    import zlib

    import numpy as np

    out = dict(_drawn_inputs(seed))
    spreads = {'L0_attn_b_proj': (0.0, 0.1)}
    factors = {'L0_ffn_Wg': 3.652, 'L0_ffn_W1': 3.188, 'L0_ffn_W2': 3.181}
    for name, (base, spread) in spreads.items():
        noise = np.random.default_rng([zlib.crc32(name.encode()), seed]).standard_normal(out[name].shape)
        drawn = base * np.exp(spread * noise) if base else spread * noise
        out[name] = jnp.asarray(drawn.astype(out[name].dtype))
    for name, factor in factors.items():
        out[name] = (out[name] * factor).astype(out[name].dtype)
    return out
```

```python
from contextlib import ExitStack

import concourse.bass as bass
from concourse import mybir

P = 128
TILES = 4
SEQ = P * TILES
DIM = 256
KT = DIM // P
HEADS = 16
HD = DIM // HEADS
GROUPS = 4
HG = HEADS // GROUPS
GP = HG * HD
STACK = 4 * HD
AUG = 2
UNITS = HG * TILES
RING = 8
EXPERTS = 8
TOPK = 2
FF = 512
FT = FF // P
SCALE = HD ** -0.5
EPS = 1e-5
ROW = DIM + 4
C_ID, C_DIFF, C_G1, C_E0 = DIM, DIM + 1, DIM + 2, DIM + 3
FAR = 1 << 20

F32 = mybir.dt.float32
F32R = mybir.dt.float32r
BF16 = mybir.dt.bfloat16
U32 = mybir.dt.uint32
ALU = mybir.AluOpType
ACT = mybir.ActivationFunctionType
AX = mybir.AxisListType

ROUNDS = [
    (0, 1, "peak3", -1), (0, 3, "logit", -2), (0, 5, "turn1", -1), (0, 7, "xT0", 1), (0, 9, "xT1", 1),
    (0, 11, "logitT", -2), (0, 13, "qk0", 1), (0, 15, "place", -2),
    (1, 1, "peak0", 0), (1, 3, "qk1", 1), (1, 5, "turn2", -1), (1, 9, "qk2", 1), (1, 13, "qk3", 1),
    (2, 1, "peak1", 0), (2, 5, "turn3", -1), (2, 9, "oT0", -1), (2, 11, "oT1", -1), (2, 13, "proj0", -1),
    (2, 15, "proj1", -1),
    (3, 1, "peak2", 0), (3, 3, "v0", 1), (3, 5, "turn0", 0), (3, 7, "v1", 1), (3, 9, "x1T0", -1),
    (3, 11, "x1T1", -1),
]
NAMES = [r[2] for r in ROUNDS]
OFFSET = {r[2]: r[3] for r in ROUNDS}
AT = {(r[0], r[1]): r[2] for r in ROUNDS}


def wait(engine, sem, value):
    if not isinstance(value, int) or value > 0:
        engine.wait_ge(sem, value)


def settle(engine, sem):
    engine.sem_inc(sem, 1)


class Iteration:

    def __init__(self, pair, odd, n_seq):
        self.b = 2 * pair + odd
        self.odd = odd % 2
        self.known = isinstance(pair, int)
        self.n_seq = n_seq

    def on(self, offset):
        return not self.known or 0 <= self.b + offset < self.n_seq

    def rounds_before(self, b, name):
        total = 0
        for c in range(-1, b + 1):
            for n in NAMES:
                if c == b and n == name:
                    return total
                total += 0 <= c + OFFSET[n] < self.n_seq
        return total

    def round(self, name, shift=0):
        if self.known:
            return self.rounds_before(self.b + shift, name)
        return len(NAMES) * (self.b + (shift - 2)) + (self.rounds_before(2, NAMES[0]) + NAMES.index(name))

    def done(self, name, shift=0):
        return self.round(name, shift) + 1


def iterations(engine, n_seq, body):
    for b in (-1, 0, 1):
        body(Iteration(b // 2, b % 2, n_seq))
    with engine.Fori(1, n_seq // 2 - 1) as pair:
        body(Iteration(pair, 0, n_seq))
        body(Iteration(pair, 1, n_seq))
    for b in range(n_seq - 2, n_seq + 2):
        body(Iteration(b // 2, b % 2, n_seq))


def attention(nc, x, w_qkv, w_proj, b_proj, w_gate, x1_dram, table):
    n_seq = x.shape[0]
    cap = table.shape[0] // EXPERTS
    n_fill = table.shape[0] // SEQ

    x_rows = x.rearrange("b (p t) c -> b p (t c)", t=TILES)
    x1_rows = x1_dram.rearrange("(b p t) c -> b p t c", p=P, t=TILES)
    table_rows = table.rearrange("(n p t) c -> n p (t c)", p=P, t=TILES)

    with ExitStack() as ctx:
        def sb(name, shape, dt=F32):
            return ctx.enter_context(nc.sbuf_tensor(name, shape, dt))

        def psum(name, shape):
            return ctx.enter_context(nc.psum_tensor(name, shape, F32))

        def sem(name):
            return ctx.enter_context(nc.semaphore(name))

        ps_rows = [psum(f"ps_rows{i}", [P, 2, SEQ]) for i in range(2)]
        ps_cols = [psum(f"ps_cols{i}", [P, SEQ]) for i in range(2)]
        ps_pv = psum("ps_pv", [P, SEQ])
        ps_m = psum("ps_m", [P, SEQ])

        ident = sb("ident", [P, P])
        before = sb("before", [P, P], BF16)
        ones = sb("ones", [P, P], BF16)
        half = sb("half", [P, TILES])
        number = sb("number", [P, EXPERTS])
        w_in = sb("w_in", [P, KT, 3 * DIM])
        w_qk = sb("w_qk", [P, KT, 4, P])
        w_out = sb("w_out", [P, KT, DIM])
        bias = sb("bias", [P, DIM])
        gate_rows = sb("gate_rows", [EXPERTS, DIM])
        gate_t = sb("gate_t", [P, KT, EXPERTS])
        zero_rows = sb("zero_rows", [2 * UNITS, P])
        blank = sb("blank", [P, TILES, ROW])

        xs = sb("xs", [P, TILES, DIM])
        xb = [sb(f"xb{i}", [P, TILES, DIM]) for i in range(2)]
        x_t = sb("x_t", [P, KT, SEQ])
        qk_hi = [sb(f"qk_hi{i}", [P, 4, SEQ], F32R) for i in range(2)]
        qk_lo = [sb(f"qk_lo{i}", [P, 4, SEQ], F32R) for i in range(2)]
        v = [sb(f"v{i}", [P, TILES, HEADS, HD + 1]) for i in range(2)]
        q_stack = [sb(f"q_stack{g}", [P, HG, SEQ], F32R) for g in range(GROUPS)]
        k_stack = [sb(f"k_stack{g}", [P, HG, SEQ], F32R) for g in range(GROUPS)]
        peak = sb("peak", [P, UNITS])
        peak_parts = [sb(f"peak_parts{i}", [P, 2 * UNITS], F32R) for i in range(2)]
        peak_rows = [sb(f"peak_rows{i}", [2 * UNITS, P]) for i in range(2)]
        probs = sb("probs", [P, RING, SEQ])
        pv = sb("pv", [P, SEQ])
        rsum = sb("rsum", [P, UNITS])
        o = sb("o", [P, TILES, DIM])
        o_t = sb("o_t", [P, KT, SEQ])
        y = sb("y", [P, TILES, DIM])
        stats = sb("stats", [P, TILES, 6])
        mv = sb("mv", [P, TILES, 2])
        var_eps = sb("var_eps", [P, TILES])
        rstd = sb("rstd", [P, TILES])
        row = sb("row", [P, TILES, ROW])
        x1_t = sb("x1_t", [P, KT, SEQ])
        logit_t = sb("logit_t", [EXPERTS, SEQ])
        logit = sb("logit", [P, TILES, EXPERTS])
        top = sb("top", [P, TILES, 8])
        top_i = sb("top_i", [P, TILES, 8], U32)
        chosen = sb("chosen", [P, TOPK, TILES])
        hot = sb("hot", [P, TOPK * TILES, EXPERTS])
        both = sb("both", [P, TILES, EXPERTS])
        count = sb("count", [P, TILES, EXPERTS])
        row_count = sb("row_count", [P, EXPERTS], BF16)
        carry = sb("carry", [P, EXPERTS], BF16)
        pos_all = sb("pos_all", [P, TILES, EXPERTS])
        hot_pos = sb("hot_pos", [P, TOPK * TILES, EXPERTS])
        pos = sb("pos", [P, TOPK * TILES])
        over = sb("over", [P, TOPK * TILES])
        slot_f = sb("slot_f", [P, TOPK * TILES])
        slot = sb("slot", [P, TOPK * TILES], U32)
        lead = sb("lead", [P, TILES])
        e_lead = sb("e_lead", [P, TILES])
        e_sum = sb("e_sum", [P, TILES])
        g0 = sb("g0", [P, TILES])
        token = sb("token", [P, TILES])

        s_const = sem("s_const")
        s_zero = sem("s_zero")
        s_weights = sem("s_weights")
        s_wqk = sem("s_wqk")
        s_blank = sem("s_blank")
        s_gate = sem("s_gate")
        s_fill = sem("s_fill")
        s_x = sem("s_x")
        s_xb = sem("s_xb")
        s_stack = [sem(f"s_stack{g}") for g in range(GROUPS)]
        s_aug = [sem(f"s_aug{g}") for g in range(GROUPS)]
        s_rows = sem("s_rows")
        s_max = sem("s_max")
        s_phi = sem("s_phi")
        s_parts = sem("s_parts")
        s_cols = sem("s_cols")
        s_exp = sem("s_exp")
        s_pv = sem("s_pv")
        s_pvout = sem("s_pvout")
        s_full = sem("s_full")
        s_free = sem("s_free")
        s_hi = sem("s_hi")
        s_rsum = sem("s_rsum")
        s_bn = sem("s_bn")
        s_pool = sem("s_pool")
        s_x1 = sem("s_x1")
        s_y = sem("s_y")
        s_route = sem("s_route")
        s_lead = sem("s_lead")
        s_slot = sem("s_slot")
        s_scatter = sem("s_scatter")

        s_waited_sp, s_waited_pool = sem("s_waited_sp"), sem("s_waited_pool")
        s_waited_pe, s_waited_dve = sem("s_waited_pe"), sem("s_waited_dve")

        ROUTE = 28
        COUNTED, LED = 15, 16

        block = ctx.enter_context(nc.Block())

        @block.sync
        def _(sp):
            sp.dma_start(xs[:].rearrange("p t c -> p (t c)"), x_rows[0]).then_inc(s_x, 16)
            sp.dma_start(w_in[:], w_qkv.rearrange("(k p) n -> p k n", p=P)).then_inc(s_weights, 16)
            sp.dma_start(w_out[:], w_proj.rearrange("(k p) n -> p k n", p=P)).then_inc(s_weights, 16)
            sp.dma_start(gate_rows[:], w_gate).then_inc(s_weights, 16)
            sp.dma_start(bias[:], b_proj.rearrange("(a n) -> a n", a=1).to_broadcast([P, DIM])).then_inc(s_weights, 16)
            sp.wait_ge(s_zero, 6)
            filled = [0]

            def fill(n):
                for i in range(filled[0], min(filled[0] + n, n_fill)):
                    if i == 0:
                        sp.wait_ge(s_blank, 2)
                    sp.dma_start(table_rows[i], blank[:].rearrange("p t c -> p (t c)")).then_inc(s_fill, 16)
                filled[0] = min(filled[0] + n, n_fill)

            def body(it):
                b = it.b
                for s in range(4):
                    g, off = (s + 1) % 4, 0 if s < 3 else 1
                    if it.on(off):
                        wait(sp, s_cols, (b + (off - 1)) * 64 + (UNITS * (g + 1)))
                        settle(sp, s_waited_sp)
                        sp.wait_ge(s_free, it.done("qk3", off - 1))
                        par = (it.odd + off) % 2
                        m, part = g // 2, slice(GP * (g % 2), GP * (g % 2) + GP)
                        hi, lo = qk_hi[par], qk_lo[par]
                        for r, (a, c) in enumerate([(hi, hi), (lo, hi), (hi, lo), (lo, lo)]):
                            rows = slice(HD * r, HD * r + HD)
                            sp.dma_start(q_stack[g][rows].bitcast(F32), a[part, m, :].bitcast(F32)).then_inc(s_stack[g], 16)
                            sp.dma_start(k_stack[g][rows].bitcast(F32), c[part, 2 + m, :].bitcast(F32)).then_inc(s_stack[g], 16)
                        sp.dma_start(q_stack[g][STACK:STACK + AUG].bitcast(F32), zero_rows[:]).then_inc(s_stack[g], 16)
                    g, off = (s - 1) % 4, 0 if s > 0 else -1
                    if it.on(off):
                        sp.wait_ge(s_free, it.done(f"peak{g}"))
                        sp.dma_start(q_stack[g][STACK:STACK + AUG].bitcast(F32), peak_rows[g % 2][:]).then_inc(s_aug[g], 16)
                    if s == 0 and it.on(-2):
                        wait(sp, s_x1, (b - 1) * TILES)
                        settle(sp, s_waited_sp)
                        sp.dma_start(x1_rows[b - 2], row[:, :, 0:DIM]).then_inc(s_y, 16)
                    if s == 3 and it.on(2):
                        sp.wait_ge(s_xb, b + 2)
                        settle(sp, s_waited_sp)
                        sp.wait_ge(s_full, it.done("xT1"))
                        settle(sp, s_waited_sp)
                        sp.dma_start(xs[:].rearrange("p t c -> p (t c)"), x_rows[b + 2]).then_inc(s_x, 16)
                    if it.known:
                        fill(8)

            iterations(sp, n_seq, body)
            sp.wait_ge(s_fill, 16 * n_fill)
            sp.wait_ge(s_y, 16 * n_seq)

        @block.gpsimd
        def _(pool):
            pool.memset(ident[:], 0.0).then_inc(s_const, 1)
            pool.memset(before[:], 1.0).then_inc(s_const, 1)
            pool.memset(ones[:], 1.0).then_inc(s_const, 1)
            pool.memset(half[:], -0.5).then_inc(s_const, 1)
            pool.memset(blank[:], 0.0).then_inc(s_blank, 1)
            pool.iota(number[:], [[1, EXPERTS]], base=0, channel_multiplier=0,
                      allow_small_or_imprecise_dtypes=True).then_inc(s_const, 1)
            pool.iota(token[:], [[1, TILES]], base=0, channel_multiplier=TILES,
                      allow_small_or_imprecise_dtypes=True).then_inc(s_const, 1)
            pool.wait_ge(s_const, 6)
            pool.affine_select(out=ident[:], in_=ident[:], compare_op=ALU.not_equal, fill=1.0, base=0,
                               pattern=[[-1, P]], channel_multiplier=1).then_inc(s_const, 1)
            pool.affine_select(out=before[:], in_=before[:], compare_op=ALU.is_gt, fill=0.0, base=0,
                               pattern=[[1, P]], channel_multiplier=-1).then_inc(s_const, 1)
            pool.wait_ge(s_blank, 1)
            pool.memset(blank[:].bitcast(U32)[:, :, C_ID:C_ID + 1], FAR).then_inc(s_blank, 1)
            pool.wait_ge(s_weights, 64)

            def body(it):
                b = it.b
                for s in range(4):
                    if s == 1 and it.on(-2):
                        pool.wait_ge(s_slot, b - 1)
                        pool.wait_ge(s_fill, 16 * n_fill)
                        settle(pool, s_waited_pool)
                        for k in range(TOPK):
                            for t in range(TILES):
                                c = k * TILES + t
                                pool.indirect_dma_start(
                                    table, bass.IndirectOffsetOnAxis(ap=slot[:, c:c + 1], axis=0), row[:, t, :], None,
                                    bounds_check=table.shape[0] - 1, oob_is_err=False).then_inc(s_scatter, 16)
                    if s == 3:
                        if it.on(1):
                            pool.wait_ge(s_x, 16 * (b + 2))
                            if it.on(-1):
                                pool.wait_ge(s_free, it.done("proj1"))
                            pool.tensor_tensor(xb[(it.odd + 1) % 2][:], xs[:],
                                               bias[:].rearrange("p (a c) -> p a c", a=1).to_broadcast([P, TILES, DIM]),
                                               ALU.add).then_inc(s_xb, 1)
                        if it.on(-1):
                            pool.wait_ge(s_bn, 8 * b)
                            settle(pool, s_waited_pool)
                            pool.tensor_scalar(var_eps[:], mv[:, :, 1], EPS, None, ALU.add).then_inc(s_pool, 1)
                            pool.wait_ge(s_pool, 2 * b - 1)
                            pool.tensor_tensor(rstd[:], var_eps[:], half[:], ALU.pow).then_inc(s_pool, 1)
                            pool.wait_ge(s_pool, 2 * b)
                            wait(pool, s_scatter, (b - 1) * (16 * TOPK * TILES))
                            wait(pool, s_y, (b - 1) * 16)
                            settle(pool, s_waited_pool)
                            for t in range(TILES):
                                pool.tensor_scalar(row[:, t, 0:DIM], y[:, t, :], mv[:, t, 0:1], rstd[:, t:t + 1],
                                                   ALU.subtract, ALU.mult).then_inc(s_x1, 1)

            iterations(pool, n_seq, body)
            pool.wait_ge(s_scatter, 16 * TOPK * TILES * n_seq)

        @block.tensor
        def _(pe):
            pe.wait_ge(s_weights, 64)
            pe.wait_ge(s_const, 8)
            pe.wait_ge(s_zero, 6)
            for k in range(KT):
                last = pe.transpose(ps_m[:, k * EXPERTS:(k + 1) * EXPERTS], gate_rows[:, k * P:(k + 1) * P],
                                    ident[0:EXPERTS, 0:EXPERTS])
            last.then_inc(s_gate, 1)
            pe.wait_ge(s_gate, 2)
            pe.wait_ge(s_wqk, 1)

            def round_(it, name):
                b = it.b
                wait(pe, s_free, it.round(name))
                kind, n = name.rstrip("0123"), int(name[-1]) if name[-1].isdigit() else 0
                if kind == "peak":
                    pe.wait_ge(s_parts, (b + OFFSET[name]) * GROUPS + (n + 1))
                    last = pe.transpose(ps_m[0:2 * UNITS, 0:P], peak_parts[n % 2][:].bitcast(F32), ident[:])
                elif kind == "xT":
                    pe.wait_ge(s_x, 16 * (b + 2))
                    for t in range(TILES):
                        last = pe.transpose(ps_m[:, t * P:(t + 1) * P], xs[:, t, n * P:(n + 1) * P], ident[:])
                elif kind == "qk":
                    for k in range(KT):
                        last = pe.matmul(ps_m[:], w_qk[:, k, n, :], x_t[:, k, :], start=k == 0, stop=k == KT - 1)
                elif kind == "v":
                    for t in range(2):
                        for k in range(KT):
                            tok = slice((2 * n + t) * P, (2 * n + t + 1) * P)
                            last = pe.matmul(ps_m[:, t * DIM:(t + 1) * DIM], x_t[:, k, tok], w_in[:, k, 2 * DIM:],
                                             start=k == 0, stop=k == KT - 1)
                elif kind == "turn":
                    pe.wait_ge(s_pvout, (b + OFFSET[name]) * GROUPS + (n + 1))
                    for t in range(TILES):
                        last = pe.transpose(ps_m[:, t * P:(t + 1) * P], pv[:, t * P:(t + 1) * P], ident[:])
                elif kind == "oT":
                    for t in range(TILES):
                        last = pe.transpose(ps_m[:, t * P:(t + 1) * P], o[:, t, n * P:(n + 1) * P], ident[:])
                elif kind == "proj":
                    for t in range(2):
                        for k in range(KT):
                            tok = slice((2 * n + t) * P, (2 * n + t + 1) * P)
                            last = pe.matmul(ps_m[:, t * DIM:(t + 1) * DIM], o_t[:, k, tok], w_out[:, k, :],
                                             start=k == 0, stop=k == KT - 1)
                elif kind == "x1T":
                    pe.wait_ge(s_x1, TILES * b)
                    for t in range(TILES):
                        last = pe.transpose(ps_m[:, t * P:(t + 1) * P], row[:, t, n * P:(n + 1) * P], ident[:])
                elif kind == "logit":
                    for k in range(KT):
                        last = pe.matmul(ps_m[0:EXPERTS, :], gate_t[:, k, :], x1_t[:, k, :], start=k == 0,
                                         stop=k == KT - 1)
                elif kind == "logitT":
                    settle(pe, s_waited_pe)
                    for t in range(TILES):
                        last = pe.transpose(ps_m[:, t * EXPERTS:(t + 1) * EXPERTS], logit_t[:, t * P:(t + 1) * P],
                                            ident[0:EXPERTS, 0:EXPERTS])
                else:
                    pe.wait_ge(s_route, (b - 2) * ROUTE + COUNTED)
                    pe.matmul(ps_m[:, 0:EXPERTS], before[:], row_count[:], start=True, stop=False)
                    last = pe.matmul(ps_m[:, 0:EXPERTS], ones[:], carry[:], start=False, stop=True)
                last.then_inc(s_full, 1)

            def body(it):
                b = it.b
                for s in range(4):
                    for j in range(UNITS):
                        if j % 2 == 0 and it.on(0):
                            n = j // 2
                            if n == 0:
                                pe.wait_ge(s_stack[s], (b + 1) * (16 * 9))
                            wait(pe, s_max, b * 32 + (8 * s + n - 1))
                            for i in range(2):
                                t = 2 * (n % 2) + i
                                last = pe.matmul(ps_rows[n % 2][:, i, :], q_stack[s][:, n // 2, t * P:(t + 1) * P],
                                                 k_stack[s][:, n // 2, :], start=True, stop=True)
                            last.then_inc(s_rows, 1)
                        g, off = (s + 2) % 4, -1 if s < 2 else 0
                        if it.on(off):
                            if j == 0:
                                pe.wait_ge(s_aug[g], (b + (off + 1)) * 16)
                            wait(pe, s_exp, (b + off) * 64 + (16 * g + j - 1))
                            t, h = j // HG, j % HG
                            pe.matmul(ps_cols[j % 2][:], k_stack[g][:, h, t * P:(t + 1) * P], q_stack[g][:, h, :],
                                      start=True, stop=True).then_inc(s_cols, 1)
                        if j % HG == 1:
                            t = j // HG - 1
                            g, off = ((s + 2) % 4, -1 if s < 2 else 0) if t >= 0 else ((s + 1) % 4, -1 if s < 3 else 0)
                            t %= TILES
                            if it.on(off):
                                if t == 0:
                                    wait(pe, s_pvout, (b + off) * GROUPS + g)
                                pe.wait_ge(s_exp, (b + off) * 64 + (16 * g + HG * (t + 1)))
                                par = (it.odd + off) % 2
                                for h in range(HG):
                                    last = pe.matmul(ps_pv[32 * h:32 * h + HD + 1, :], v[par][:, t, HG * g + h, :],
                                                     probs[:, (HG * t + h) % RING, :], start=t == 0, stop=t == TILES - 1)
                                last.then_inc(s_pv, 1)
                        name = AT.get((s, j))
                        if name and it.on(OFFSET[name]):
                            round_(it, name)

            iterations(pe, n_seq, body)

        @block.scalar
        def _(act):
            def body(it):
                b = it.b

                def full(name):
                    act.wait_ge(s_full, it.done(name))

                def copy_out(name, out, in_):
                    full(name)
                    act.copy(out, in_).then_inc(s_free, 1)

                for s in range(4):
                    for j in range(UNITS):
                        g, off = (s + 2) % 4, -1 if s < 2 else 0
                        if it.on(off):
                            if j % HG == 0:
                                wait(act, s_pv, (b + off) * 16 + (4 * g + j // HG - 1))
                            act.wait_ge(s_cols, (b + off) * 64 + (16 * g + j + 1))
                            act.activation(probs[:, j % RING, :], ps_cols[j % 2][:], ACT.Exp,
                                           scale=SCALE).then_inc(s_exp, 1)
                        name = AT.get((s, j - 1))
                        if name and it.on(OFFSET[name]):
                            kind, n = name.rstrip("0123"), int(name[-1]) if name[-1].isdigit() else 0
                            if kind == "peak":
                                beta = b + OFFSET[name]
                                if n >= 2:
                                    act.wait_ge(s_aug[n - 2], (beta + 1) * 16)
                                else:
                                    wait(act, s_aug[n + 2], beta * 16)
                                copy_out(name, peak_rows[n % 2][:], ps_m[0:2 * UNITS, 0:P])
                            elif kind == "xT":
                                copy_out(name, x_t[:, n, :], ps_m[:])
                            elif kind == "qk":
                                full(name)
                                act.copy(qk_hi[(it.odd + 1) % 2][:, n, :], ps_m[:]).then_inc(s_hi, 1)
                            elif kind == "v":
                                copy_out(name, v[(it.odd + 1) % 2][:, 2 * n:2 * n + 2, :, 0:HD],
                                         ps_m[:].rearrange("p (t h d) -> p t h d", t=2, h=HEADS))
                            elif kind == "oT":
                                copy_out(name, o_t[:, n, :], ps_m[:])
                            elif kind == "x1T":
                                copy_out(name, x1_t[:, n, :], ps_m[:])
                            elif kind == "logit":
                                copy_out(name, logit_t[:], ps_m[0:EXPERTS, :])
                        if j == 2:
                            g, off = (s + 1) % 4, -1 if s < 3 else 0
                            if it.on(off):
                                act.wait_ge(s_pv, (b + off) * 16 + (4 * g + 4))
                                before_ = {0: ("turn0", -1), 1: ("turn1", 0), 2: ("turn2", 0), 3: ("turn3", 0)}[s]
                                if not it.known or (it.b + off) * 4 + g > 0:
                                    act.wait_ge(s_full, it.done(*before_))
                                act.copy(pv[:], ps_pv[:]).then_inc(s_pvout, 1)
                        if s == 0 and j == 15 and it.on(-2):
                            act.wait_ge(s_route, (b - 2) * ROUTE + LED)
                            act.activation(e_lead[:], lead[:], ACT.Exp).then_inc(s_lead, 1)

            iterations(act, n_seq, body)

        @block.vector
        def _(dve):
            for g in range(GROUPS):
                dve.memset(q_stack[g][:].bitcast(F32), 0.0)
                last = dve.memset(k_stack[g][:].bitcast(F32), 0.0)
            last.then_inc(s_zero, 1)
            dve.memset(zero_rows[:], 0.0).then_inc(s_zero, 1)
            dve.memset(ps_pv[:], 0.0).then_inc(s_zero, 1)
            for i in range(2):
                last = dve.memset(v[i][:, :, :, HD:HD + 1], 1.0)
            last.then_inc(s_zero, 1)
            dve.memset(carry[:], 0.0).then_inc(s_zero, 1)
            dve.memset(count[:, 0, :], 0.0)
            dve.wait_ge(s_zero, 5)
            for g in range(GROUPS):
                last = dve.memset(k_stack[g][STACK:STACK + AUG].bitcast(F32), 1.0)
            last.then_inc(s_zero, 1)
            dve.wait_ge(s_weights, 64)
            for m in range(4):
                for g in range(2):
                    src = w_in[:, :, m * P + g * GP:m * P + (g + 1) * GP].rearrange("p k (h r) -> p k r h", h=HG)
                    for k in range(KT):
                        last = dve.tensor_copy(w_qk[:, k, m, g * GP:(g + 1) * GP].rearrange("p (r h) -> p r h", h=HG),
                                               src[:, k])
            last.then_inc(s_wqk, 1)
            dve.wait_ge(s_gate, 1)
            dve.tensor_copy(gate_t[:].rearrange("p k e -> p (k e)"), ps_m[:, 0:KT * EXPERTS]).then_inc(s_gate, 1)

            def body(it):
                b = it.b

                def full(name):
                    dve.wait_ge(s_full, it.done(name))

                def turn(name, g):
                    beta = b + OFFSET[name]
                    full(name)
                    parts = ps_m[:].rearrange("p (u d) -> p u d", d=32)
                    dve.reciprocal(rsum[:], parts[:, :, HD]).then_inc(s_rsum, 1)
                    dve.wait_ge(s_rsum, beta * GROUPS + (g + 1))
                    dve.tensor_tensor(
                        o[:, :, g * GP:(g + 1) * GP].rearrange("p t (h d) -> p t h d", h=HG),
                        ps_m[:].rearrange("p (t h d) -> p t h d", t=TILES, h=HG)[:, :, :, 0:HD],
                        rsum[:].rearrange("p (t h a) -> p t h a", t=TILES, a=1).to_broadcast([P, TILES, HG, HD]),
                        ALU.mult).then_inc(s_free, 1)

                def low_part(n):
                    par = (it.odd + 1) % 2
                    dve.wait_ge(s_hi, (b + 1) * 4 + (n + 1))
                    dve.tensor_tensor(qk_lo[par][:, n, :], ps_m[:], qk_hi[par][:, n, :].bitcast(F32),
                                      ALU.subtract).then_inc(s_free, 1)

                def project(n):
                    beta = b - 1
                    full(f"proj{n}")
                    tt = slice(2 * n, 2 * n + 2)
                    if n == 0:
                        wait(dve, s_x1, beta * TILES)
                    dve.tensor_tensor(y[:, tt, :], ps_m[:].rearrange("p (t c) -> p t c", t=2),
                                      xb[(it.odd + 1) % 2][:, tt, :], ALU.add).then_inc(s_free, 1)
                    dve.wait_ge(s_free, it.done(f"proj{n}"))
                    for t in (2 * n, 2 * n + 1):
                        dve.bn_stats(stats[:, t, :], y[:, t, :]).then_inc(s_bn, 1)
                    for t in (2 * n, 2 * n + 1):
                        dve.wait_ge(s_bn, beta * 8 + (4 * n + t - 2 * n + 1))
                        settle(dve, s_waited_dve)
                        dve.bn_aggr(mv[:, t, :], stats[:, t, :]).then_inc(s_bn, 1)

                link_no = [0]

                def link(ins):
                    link_no[0] += 1
                    ins.then_inc(s_route, 1)
                    dve.wait_ge(s_route, (b - 2) * ROUTE + link_no[0])

                def route_first():
                    full("logitT")
                    dve.tensor_copy(logit[:].rearrange("p t e -> p (t e)"),
                                    ps_m[:, 0:TILES * EXPERTS]).then_inc(s_free, 1)
                    dve.wait_ge(s_free, it.done("logitT"))
                    settle(dve, s_waited_dve)
                    for t in range(TILES):
                        last = dve.max(top[:, t, :], logit[:, t, :])
                        if t < TILES - 1:
                            last.then_inc(s_route, 1)
                            link_no[0] += 1
                    link(last)
                    settle(dve, s_waited_dve)
                    for t in range(TILES):
                        last = dve.max_index(top_i[:, t, :], top[:, t, :], logit[:, t, :])
                        if t < TILES - 1:
                            last.then_inc(s_route, 1)
                            link_no[0] += 1
                    link(last)
                    link(dve.tensor_copy(chosen[:], top_i[:, :, 0:TOPK].rearrange("p t k -> p k t")))
                    link(dve.tensor_tensor(
                        hot[:], number[:].rearrange("p (a e) -> p a e", a=1).to_broadcast([P, TOPK * TILES, EXPERTS]),
                        chosen[:].rearrange("p k (t a) -> p (k t) a", a=1).to_broadcast([P, TOPK * TILES, EXPERTS]),
                        ALU.is_equal))
                    link(dve.tensor_tensor(both[:], hot[:, 0:TILES, :], hot[:, TILES:, :], ALU.add))
                    for t in range(1, TILES):
                        link(dve.tensor_tensor(count[:, t, :], count[:, t - 1, :], both[:, t - 1, :], ALU.add))
                    link(dve.tensor_tensor(row_count[:], count[:, TILES - 1, :], both[:, TILES - 1, :], ALU.add))
                    link(dve.tensor_tensor(lead[:], top[:, :, 1], top[:, :, 0], ALU.subtract))

                def route_second():
                    full("place")
                    base = ps_m[:, 0:EXPERTS].rearrange("p (a e) -> p a e", a=1).to_broadcast([P, TILES, EXPERTS])
                    dve.tensor_tensor(pos_all[:], count[:], base, ALU.add).then_inc(s_free, 1)
                    dve.wait_ge(s_free, it.done("place"))
                    link(dve.tensor_tensor(carry[:], carry[:], row_count[:], ALU.add))
                    for k in range(TOPK):
                        link(dve.tensor_tensor(hot_pos[:, k * TILES:(k + 1) * TILES, :],
                                               hot[:, k * TILES:(k + 1) * TILES, :], pos_all[:], ALU.mult))
                    link(dve.tensor_reduce(pos[:], hot_pos[:], AX.X, ALU.add))
                    link(dve.tensor_scalar(over[:], pos[:], float(cap), float(FAR), ALU.is_ge, ALU.mult))
                    link(dve.scalar_tensor_tensor(slot_f[:], chosen[:].rearrange("p k t -> p (k t)"), float(cap),
                                                  pos[:], ALU.mult, ALU.add))
                    wait(dve, s_scatter, (b - 2) * (16 * TOPK * TILES))
                    link(dve.tensor_tensor(slot[:], slot_f[:], over[:], ALU.add))
                    dve.wait_ge(s_lead, b - 1)
                    link(dve.tensor_scalar(e_sum[:], e_lead[:], 1.0, None, ALU.add))
                    link(dve.reciprocal(g0[:], e_sum[:]))
                    link(dve.tensor_tensor(row[:, :, C_G1], e_lead[:], g0[:], ALU.mult))
                    link(dve.tensor_tensor(row[:, :, C_DIFF], g0[:], row[:, :, C_G1], ALU.subtract))
                    dve.tensor_copy(row[:, :, C_E0], chosen[:, 0, :])
                    link(dve.tensor_copy(row[:].bitcast(U32)[:, :, C_ID], token[:]))
                    dve.tensor_scalar(token[:], token[:], float(SEQ), None, ALU.add).then_inc(s_slot, 1)

                for s in range(4):
                    for j in range(UNITS):
                        if s == 1 and j == 0 and it.on(-2):
                            route_second()
                        if j % 2 and it.on(0):
                            n = j // 2
                            dve.wait_ge(s_rows, b * 32 + (8 * s + n + 1))
                            if n == 0:
                                wait(dve, s_parts, b * GROUPS + s)
                            dve.tensor_reduce(peak[:, 2 * n:2 * n + 2], ps_rows[n % 2][:], AX.X, ALU.max,
                                              negate=True).then_inc(s_max, 1)
                        if j == 15 and it.on(0):
                            prev = (("peak2", -1), ("peak3", 0), ("peak0", 0), ("peak1", 0))[s]
                            if not it.known or it.b > 0 or s >= 2:
                                dve.wait_ge(s_full, it.done(*prev))
                            dve.wait_ge(s_max, b * 32 + (8 * s + 8))
                            parts = peak_parts[s % 2]
                            dve.tensor_copy(parts[:, 0:UNITS], peak[:]).then_inc(s_phi, 1)
                            dve.wait_ge(s_phi, b * GROUPS + (s + 1))
                            dve.tensor_tensor(parts[:, UNITS:], peak[:], parts[:, 0:UNITS].bitcast(F32),
                                              ALU.subtract).then_inc(s_parts, 1)
                        if j == 6 and s < 3 and it.on(-1):
                            turn(f"turn{s + 1}", s + 1)
                        if j == 6 and s == 3 and it.on(0):
                            turn("turn0", 0)
                        if it.on(1) and (s, j) in ((0, 15), (1, 5), (1, 11), (1, 15)):
                            low_part({(0, 15): 0, (1, 5): 1, (1, 11): 2, (1, 15): 3}[s, j])
                        if s == 0 and j == 12 and it.on(-2):
                            route_first()
                        if s == 2 and j == 14 and it.on(-1):
                            project(0)
                        if s == 3 and j == 0 and it.on(-1):
                            project(1)

            iterations(dve, n_seq, body)


def experts(nc, table, w1, w2, x1_dram):
    cap = table.shape[0] // EXPERTS
    per = cap // SEQ
    n_chunks = EXPERTS * per
    n_tokens = x1_dram.shape[0]
    assert cap % SEQ == 0 and per % 2 == 0 and EXPERTS % 2 == 0 and EXPERTS > 4 and per > 2
    chunk_rows = table.rearrange("(n p t) c -> n p (t c)", p=P, t=TILES)
    w1_rows = w1.rearrange("e (k p) f -> e p k f", p=P)
    w2_rows = w2.rearrange("e (k p) d -> e p k d", p=P)

    with ExitStack() as ctx:
        def sb(name, shape, dt=F32):
            return ctx.enter_context(nc.sbuf_tensor(name, shape, dt))

        def psum(name, shape):
            return ctx.enter_context(nc.psum_tensor(name, shape, F32))

        def sem(name):
            return ctx.enter_context(nc.semaphore(name))

        ps_turn = [psum(f"ps_turn{i}", [P, SEQ]) for i in range(KT)]
        ps_hid = [psum(f"ps_hid{i}", [P, 2, SEQ]) for i in range(2)]
        ps_out = psum("ps_out", [P, TILES, DIM])

        ident = sb("ident_e", [P, P])
        rows = [sb(f"rows{i}", [P, TILES, ROW]) for i in range(2)]
        x_hi = [sb(f"x_hi{i}", [P, KT, SEQ], F32R) for i in range(2)]
        x_lo = [sb(f"x_lo{i}", [P, KT, SEQ], F32R) for i in range(2)]
        raw1 = sb("raw1", [P, KT, 2 * FF])
        raw2 = sb("raw2", [P, FT, DIM])
        w1_hi = [sb(f"w1_hi{i}", [P, KT, 2 * FF], F32R) for i in range(2)]
        w1_lo = [sb(f"w1_lo{i}", [P, KT, 2 * FF], F32R) for i in range(2)]
        w2_hi = [sb(f"w2_hi{i}", [P, FT, DIM], F32R) for i in range(2)]
        w2_lo = [sb(f"w2_lo{i}", [P, FT, DIM], F32R) for i in range(2)]
        act_in = [sb(f"act_in{i}", [P, SEQ]) for i in range(2)]
        hid = [sb(f"hid{i}", [P, SEQ]) for i in range(2)]
        h_hi = [sb(f"h_hi{i}", [P, FT, SEQ], F32R) for i in range(2)]
        h_lo = [sb(f"h_lo{i}", [P, FT, SEQ], F32R) for i in range(2)]
        out = [sb(f"out{i}", [P, TILES, DIM]) for i in range(2)]
        gate = [sb(f"gate{i}", [P, TILES]) for i in range(2)]
        gate_part = sb("gate_part", [P, TILES])
        token = [sb(f"token{i}", [P, TILES], U32) for i in range(2)]
        expert_no = sb("expert_no", [P, 1])

        s_ident = sem("s_ident")
        s_rows = [sem(f"s_rows{i}") for i in range(2)]
        s_raw = sem("s_raw")
        s_whi = sem("s_whi")
        s_w = sem("s_w")
        s_turn = sem("s_turn")
        s_xhi = sem("s_xhi")
        s_xlo = sem("s_xlo")
        s_hid = sem("s_hid")
        s_gelu = sem("s_gelu")
        s_mul = sem("s_mul")
        s_hhi = sem("s_hhi")
        s_hlo = sem("s_hlo")
        s_out = sem("s_out")
        s_gp = sem("s_gp")
        s_meta = sem("s_meta")
        s_scaled = sem("s_scaled")
        s_add = sem("s_add")
        s_eno = sem("s_eno")

        s_waited_sp, s_waited_pool = sem("s_waited_sp_e"), sem("s_waited_pool_e")

        W_PIECES = 3
        ADDED = 16 * TILES

        class Chunk:

            def __init__(self, e, par, lead, half, odd, last=False):
                self.e, self.par, self.lead, self.half, self.odd, self.last = e, par, lead, half, odd, last
                self.n = half * 2 + odd
                self.first = isinstance(half, int) and self.n == 0
                self.final_expert = isinstance(e, int) and e == EXPERTS - 1

        def chunks(engine, body):
            halves = per // 2

            def expert(e, par, final=False):
                for odd in range(2):
                    body(Chunk(e, par, True, e * halves, odd))
                with engine.Fori(1, halves - 1 if final else halves) as i:
                    for odd in range(2):
                        body(Chunk(e, par, False, e * halves + i, odd))
                if final:
                    for odd in range(2):
                        body(Chunk(e, par, False, e * halves + halves - 1, odd, last=True))

            expert(0, 0)
            expert(1, 1)
            with engine.Fori(1, EXPERTS // 2 - 1) as pair:
                expert(pair * 2, 0)
                expert(pair * 2 + 1, 1)
            expert(EXPERTS - 2, 0)
            expert(EXPERTS - 1, 1, final=True)

        def pieces(par):
            return [(raw1[:, 0], w1_hi[par][:, 0], w1_lo[par][:, 0]), (raw1[:, 1], w1_hi[par][:, 1], w1_lo[par][:, 1]),
                    (raw2[:], w2_hi[par][:], w2_lo[par][:])]

        block = ctx.enter_context(nc.Block())

        @block.sync
        def _(sp):
            def load_rows(odd, n):
                sp.dma_start(rows[odd][:].rearrange("p t c -> p (t c)"), chunk_rows[n]).then_inc(s_rows[odd], 16)

            def load_weights(e):
                sp.dma_start(raw1[:], w1_rows[e]).then_inc(s_raw, 16)
                sp.dma_start(raw2[:], w2_rows[e]).then_inc(s_raw, 16)

            load_rows(0, 0)
            load_weights(0)
            load_rows(1, 1)

            def body(k):
                if k.lead and k.odd and not k.final_expert:
                    sp.wait_ge(s_w, k.e * W_PIECES + W_PIECES)
                    settle(sp, s_waited_sp)
                    load_weights(k.e + 1)
                if not k.last:
                    sp.wait_ge(s_turn, k.n * KT + KT)
                    settle(sp, s_waited_sp)
                    sp.wait_ge(s_meta, k.n + 1)
                    settle(sp, s_waited_sp)
                    load_rows(k.odd, k.n + 2)

            chunks(sp, body)
            sp.wait_ge(s_add, n_chunks * ADDED)

        @block.gpsimd
        def _(pool):
            pool.memset(ident[:], 0.0).then_inc(s_ident, 1)
            pool.wait_ge(s_ident, 1)
            pool.affine_select(out=ident[:], in_=ident[:], compare_op=ALU.not_equal, fill=1.0, base=0,
                               pattern=[[-1, P]], channel_multiplier=1).then_inc(s_ident, 1)

            def add_out(buf, n):
                pool.wait_ge(s_scaled, n * TILES + TILES)
                wait(pool, s_add, n * ADDED)
                settle(pool, s_waited_pool)
                for t in range(TILES):
                    pool.indirect_dma_start(
                        x1_dram, bass.IndirectOffsetOnAxis(ap=token[buf][:, t:t + 1], axis=0), out[buf][:, t, :], None,
                        bounds_check=n_tokens - 1, oob_is_err=False, compute_op=ALU.add).then_inc(s_add, 16)

            def body(k):
                if not k.first:
                    add_out(1 - k.odd, k.n - 1)
                if k.lead and k.odd and not k.final_expert:
                    pool.wait_ge(s_raw, k.e * 32 + 64)
                    wait(pool, s_out, k.e * per)
                    settle(pool, s_waited_pool)
                    for i, (raw, hi, lo) in enumerate(pieces(1 - k.par)):
                        pool.tensor_copy(hi, raw).then_inc(s_whi, 1)
                        pool.wait_ge(s_whi, k.e * W_PIECES + (W_PIECES + i + 1))
                        pool.tensor_tensor(lo, raw, hi.bitcast(F32), ALU.subtract).then_inc(s_w, 1)

            chunks(pool, body)
            add_out((n_chunks - 1) % 2, n_chunks - 1)

        @block.tensor
        def _(pe):
            def turn(buf, n):
                for k in range(KT):
                    wait(pe, s_xlo, n * KT + (k + 1 - KT))
                    for t in range(TILES):
                        last = pe.transpose(ps_turn[k][:, t * P:(t + 1) * P], rows[buf][:, t, k * P:(k + 1) * P],
                                            ident[:])
                    last.then_inc(s_turn, 1)

            def hidden(c, f):
                wait(pe, s_mul, c.n * FT + (f - 1))
                for part in range(2):
                    cols = slice(part * FF + f * P, part * FF + (f + 1) * P)
                    i = 0
                    for k in range(KT):
                        for w, xx in ((w1_hi, x_hi), (w1_lo, x_hi), (w1_hi, x_lo)):
                            last = pe.matmul(ps_hid[f % 2][:, part, :], w[c.par][:, k, cols], xx[c.odd][:, k, :],
                                             start=i == 0, stop=i == 3 * KT - 1)
                            i += 1
                last.then_inc(s_hid, 1)

            def output(par, buf, n):
                wait(pe, s_scaled, n * TILES)
                pe.wait_ge(s_hlo, n * FT + FT)
                for t in range(TILES):
                    i = 0
                    for f in range(FT):
                        for hh, w in ((h_hi, w2_hi), (h_hi, w2_lo), (h_lo, w2_hi)):
                            last = pe.matmul(ps_out[:, t, :], hh[buf][:, f, t * P:(t + 1) * P], w[par][:, f, :],
                                             start=i == 0, stop=i == 3 * FT - 1)
                            i += 1
                last.then_inc(s_out, 1)

            pe.wait_ge(s_ident, 2)
            pe.wait_ge(s_rows[0], 16)
            turn(0, 0)

            def body(k):
                if not (k.last and k.odd):
                    pe.wait_ge(s_rows[1 - k.odd], (k.half + (k.odd + 1)) * 16)
                    turn(1 - k.odd, k.n + 1)
                if k.lead and not k.odd:
                    pe.wait_ge(s_w, k.e * W_PIECES + W_PIECES)
                pe.wait_ge(s_xlo, k.n * KT + KT)
                hidden(k, 0)
                hidden(k, 1)
                if not k.first:
                    output(1 - k.par if k.lead and not k.odd else k.par, 1 - k.odd, k.n - 1)
                hidden(k, 2)
                hidden(k, 3)

            chunks(pe, body)
            output(1, (n_chunks - 1) % 2, n_chunks - 1)

        @block.scalar
        def _(act):
            for i, (raw, hi, _) in enumerate(pieces(0)):
                act.wait_ge(s_raw, 32)
                act.copy(hi, raw).then_inc(s_whi, 1)

            def high_x(buf, n):
                for k in range(KT):
                    act.wait_ge(s_turn, n * KT + (k + 1))
                    act.copy(x_hi[buf][:, k, :], ps_turn[k][:]).then_inc(s_xhi, 1)

            def gelu(c, f):
                act.wait_ge(s_hid, c.n * FT + (f + 1))
                act.activation(act_in[f % 2][:], ps_hid[f % 2][:, 0, :], ACT.Gelu).then_inc(s_gelu, 1)

            def high_h(c, f):
                if f == 0:
                    wait(act, s_out, c.n - 1)
                act.wait_ge(s_mul, c.n * FT + (f + 1))
                act.copy(h_hi[c.odd][:, f, :], hid[f % 2][:]).then_inc(s_hhi, 1)

            def scale(buf, n):
                act.wait_ge(s_out, n + 1)
                act.wait_ge(s_meta, n + 1)
                wait(act, s_add, n * ADDED - ADDED)
                for t in range(TILES):
                    act.activation(out[buf][:, t, :], ps_out[:, t, :], ACT.Copy,
                                   scale=gate[buf][:, t:t + 1]).then_inc(s_scaled, 1)

            high_x(0, 0)

            def body(k):
                if not (k.last and k.odd):
                    high_x(1 - k.odd, k.n + 1)
                gelu(k, 0)
                gelu(k, 1)
                high_h(k, 0)
                high_h(k, 1)
                if not k.first:
                    scale(1 - k.odd, k.n - 1)
                gelu(k, 2)
                gelu(k, 3)
                high_h(k, 2)
                high_h(k, 3)

            chunks(act, body)
            scale((n_chunks - 1) % 2, n_chunks - 1)

        @block.vector
        def _(dve):
            dve.memset(expert_no[:], -1.0).then_inc(s_eno, 1)
            for i, (raw, hi, lo) in enumerate(pieces(0)):
                dve.wait_ge(s_whi, i + 1)
                dve.tensor_tensor(lo, raw, hi.bitcast(F32), ALU.subtract).then_inc(s_w, 1)

            def low_x(buf, n):
                for k in range(KT):
                    dve.wait_ge(s_xhi, n * KT + (k + 1))
                    dve.tensor_tensor(x_lo[buf][:, k, :], ps_turn[k][:], x_hi[buf][:, k, :].bitcast(F32),
                                      ALU.subtract).then_inc(s_xlo, 1)

            def product(c, f):
                dve.wait_ge(s_gelu, c.n * FT + (f + 1))
                wait(dve, s_hlo, c.n * FT + (f - 1))
                dve.tensor_tensor(hid[f % 2][:], ps_hid[f % 2][:, 1, :], act_in[f % 2][:],
                                  ALU.mult).then_inc(s_mul, 1)

            def low_h(c, f):
                dve.wait_ge(s_hhi, c.n * FT + (f + 1))
                dve.tensor_tensor(h_lo[c.odd][:, f, :], hid[f % 2][:], h_hi[c.odd][:, f, :].bitcast(F32),
                                  ALU.subtract).then_inc(s_hlo, 1)

            def meta(c):
                if c.lead and not c.odd:
                    dve.wait_ge(s_eno, c.e + 1)
                    dve.tensor_scalar(expert_no[:], expert_no[:], 1.0, None, ALU.add).then_inc(s_eno, 1)
                dve.wait_ge(s_eno, c.e + 2)
                wait(dve, s_scaled, c.n * TILES - TILES)
                wait(dve, s_add, c.n * ADDED - ADDED)
                r = rows[c.odd]
                dve.scalar_tensor_tensor(gate_part[:], r[:, :, C_E0], expert_no[:, 0:1], r[:, :, C_DIFF],
                                         ALU.is_equal, ALU.mult).then_inc(s_gp, 1)
                dve.wait_ge(s_gp, c.n + 1)
                dve.tensor_tensor(gate[c.odd][:], gate_part[:], r[:, :, C_G1], ALU.add)
                dve.tensor_copy(token[c.odd][:], r[:].bitcast(U32)[:, :, C_ID]).then_inc(s_meta, 1)

            low_x(0, 0)

            def body(k):
                if not (k.last and k.odd):
                    low_x(1 - k.odd, k.n + 1)
                product(k, 0)
                product(k, 1)
                low_h(k, 0)
                low_h(k, 1)
                dve.wait_ge(s_rows[k.odd], (k.half + 1) * 16)
                meta(k)
                product(k, 2)
                product(k, 3)
                low_h(k, 2)
                low_h(k, 3)

            chunks(dve, body)


def final_norm(nc, y_dram, out_dram):
    RING_Y = 4
    n_chunks = y_dram.shape[0] // SEQ
    y_rows = y_dram.rearrange("(n p t) c -> n p (t c)", p=P, t=TILES)
    out_rows = out_dram.rearrange("(n p t) c -> n p (t c)", p=P, t=TILES)
    with ExitStack() as ctx:
        def sb(name, shape, dt=F32):
            return ctx.enter_context(nc.sbuf_tensor(name, shape, dt))

        def sem(name):
            return ctx.enter_context(nc.semaphore(name))

        y = [sb(f"fy{i}", [P, TILES, DIM]) for i in range(RING_Y)]
        z = [sb(f"fz{i}", [P, TILES, DIM]) for i in range(RING_Y)]
        stats = [sb(f"fstats{i}", [P, TILES, 6]) for i in range(RING_Y)]
        mv = [sb(f"fmv{i}", [P, TILES, 2]) for i in range(RING_Y)]
        var_eps = [sb(f"fvar{i}", [P, TILES]) for i in range(RING_Y)]
        rstd = [sb(f"frstd{i}", [P, TILES]) for i in range(RING_Y)]
        half = sb("fhalf", [P, TILES])
        s_in = [sem(f"s_in{i}") for i in range(RING_Y)]
        s_store = [sem(f"s_store{i}") for i in range(RING_Y)]
        s_half = sem("s_fhalf")
        s_bn = sem("s_fbn")
        s_eps = sem("s_feps")
        s_rstd = sem("s_frstd")
        s_norm = sem("s_fnorm")

        s_waited_sp, s_waited_act = sem("s_waited_sp_f"), sem("s_waited_act_f")
        s_waited_pool, s_waited_dve = sem("s_waited_pool_f"), sem("s_waited_dve_f")

        def rings(engine, body):
            for r in range(RING_Y):
                body(r, r, 0)
            with engine.Fori(1, n_chunks // RING_Y) as q:
                for r in range(RING_Y):
                    body(q * RING_Y + r, r, q)

        block = ctx.enter_context(nc.Block())

        @block.sync
        def _(sp):
            def body(i, r, q):
                wait(sp, s_norm, i * TILES - (RING_Y - 1) * TILES)
                if not isinstance(i, int):
                    settle(sp, s_waited_sp)
                sp.dma_start(y[r][:].rearrange("p t c -> p (t c)"), y_rows[i]).then_inc(s_in[r], 16)

            rings(sp, body)

        @block.scalar
        def _(act):
            def body(i, r, q):
                act.wait_ge(s_norm, i * TILES + TILES)
                settle(act, s_waited_act)
                act.dma_start(out_rows[i], z[r][:].rearrange("p t c -> p (t c)")).then_inc(s_store[r], 16)

            rings(act, body)
            for r in range(RING_Y):
                act.wait_ge(s_store[r], 16 * (n_chunks // RING_Y))

        @block.gpsimd
        def _(pool):
            pool.memset(half[:], -0.5).then_inc(s_half, 1)
            pool.wait_ge(s_half, 1)

            def body(i, r, q):
                pool.wait_ge(s_bn, i * 8 + 8)
                wait(pool, s_norm, i * TILES - (RING_Y - 1) * TILES)
                settle(pool, s_waited_pool)
                pool.tensor_scalar(var_eps[r][:], mv[r][:, :, 1], EPS, None, ALU.add).then_inc(s_eps, 1)
                pool.wait_ge(s_eps, i + 1)
                pool.tensor_tensor(rstd[r][:], var_eps[r][:], half[:], ALU.pow).then_inc(s_rstd, 1)

            rings(pool, body)

        @block.vector
        def _(dve):
            def statistics(i, r, q):
                dve.wait_ge(s_in[r], q * 16 + 16)
                for t in range(TILES):
                    dve.bn_stats(stats[r][:, t, :], y[r][:, t, :]).then_inc(s_bn, 1)
                for t in range(TILES):
                    dve.wait_ge(s_bn, i * 8 + (t + 1))
                    settle(dve, s_waited_dve)
                    dve.bn_aggr(mv[r][:, t, :], stats[r][:, t, :]).then_inc(s_bn, 1)

            def normalise(i, r, q):
                dve.wait_ge(s_rstd, i + 1)
                wait(dve, s_store[r], q * 16)
                for t in range(TILES):
                    dve.tensor_scalar(z[r][:, t, :], y[r][:, t, :], mv[r][:, t, 0:1], rstd[r][:, t:t + 1],
                                      ALU.subtract, ALU.mult).then_inc(s_norm, 1)

            def body(i, r, q):
                statistics(i, r, q)
                if isinstance(q, int):
                    if r:
                        normalise(i - 1, r - 1, 0)
                elif r:
                    normalise(i - 1, r - 1, q)
                else:
                    normalise(i - 1, RING_Y - 1, q - 1)

            rings(dve, body)
            normalise(n_chunks - 1, RING_Y - 1, n_chunks // RING_Y - 1)


def transformer_layer(nc, x, w_qkv, w_proj, b_proj, w_gate, w1, w2, out):
    n_tokens = x.shape[0] * x.shape[1]
    cap = n_tokens * TOPK * 5 // 4 // EXPERTS
    x1 = nc.dram_tensor("x1", [n_tokens, DIM], F32).ap()
    table = nc.dram_tensor("expert_rows", [EXPERTS * cap, ROW], F32).ap()
    attention(nc, x, w_qkv, w_proj, b_proj, w_gate, x1, table)
    experts(nc, table, w1, w2, x1)
    final_norm(nc, x1, out.rearrange("b s c -> (b s) c"))


_INS = ["L0_attn_x", "L0_attn_w_qkv", "L0_attn_w_proj", "L0_attn_b_proj", "L0_ffn_Wg", "L0_ffn_W1", "L0_ffn_W2"]


def kernel(**inputs):
    import concourse.bacc as _bacc
    import numpy as _np
    from concourse.bass_utils import run_bass_kernel_spmd as _run

    nc = _bacc.Bacc("TRN2", target_bir_lowering=False, num_devices=1)
    arrays, args = {}, []
    for name in _INS:
        a = _np.ascontiguousarray(inputs[name])
        arrays[f"in_{name}"] = a
        args.append(nc.dram_tensor(f"in_{name}", a.shape, mybir.dt.from_np(a.dtype), kind="ExternalInput").ap())
    shape = inputs["L0_attn_x"].shape
    args.append(nc.dram_tensor("out_0", shape, F32, kind="ExternalOutput").ap())
    transformer_layer(nc, *args)
    r = _run(nc, [arrays], core_ids=[0])
    return r.results[0]["out_0"]
```

```python
from contextlib import ExitStack

import concourse.bass as bass
from concourse import mybir

P = 128
TILES = 4
SEQ = P * TILES
DIM = 256
KT = DIM // P
HEADS = 16
HD = DIM // HEADS
GROUPS = 4
HG = HEADS // GROUPS
GP = HG * HD
STACK = 4 * HD
AUG = 2
UNITS = HG * TILES
ALL = GROUPS * UNITS
RING = 8
ROWS = 3
EXPERTS = 8
TOPK = 2
FF = 512
FT = FF // P
SCALE = HD ** -0.5
EPS = 1e-5
ROW = DIM + 4
C_ID, C_DIFF, C_G1, C_E0 = DIM, DIM + 1, DIM + 2, DIM + 3
FAR = 1 << 20

F32 = mybir.dt.float32
F32R = mybir.dt.float32r
BF16 = mybir.dt.bfloat16
U32 = mybir.dt.uint32
ALU = mybir.AluOpType
ACT = mybir.ActivationFunctionType
AX = mybir.AxisListType

ROUNDS = [
    (0, 1, "x1T0", -2), (0, 3, "x1T1", -2), (0, 5, "peak3", -1), (0, 7, "turn1", -1), (0, 9, "xT0", 1),
    (0, 11, "logit", -2), (0, 13, "xT1", 1), (0, 15, "logitT", -2),
    (1, 3, "qk0", 1), (1, 5, "peak0", 0), (1, 7, "turn2", -1), (1, 11, "qk1", 1), (1, 13, "place", -2),
    (1, 15, "qk2", 1),
    (2, 3, "qk3", 1), (2, 5, "peak1", 0), (2, 7, "turn3", -1), (2, 11, "oT0", -1), (2, 13, "oT1", -1),
    (2, 15, "proj0", -1),
    (3, 3, "proj1", -1), (3, 5, "peak2", 0), (3, 7, "turn0", 0), (3, 11, "v0", 1), (3, 15, "v1", 1),
]
NAMES = [r[2] for r in ROUNDS]
OFFSET = {r[2]: r[3] for r in ROUNDS}
AT = {(r[0], r[1]): r[2] for r in ROUNDS}


def wait(engine, sem, value):
    if not isinstance(value, int) or value > 0:
        engine.wait_ge(sem, value)


def settle(engine, sem):
    engine.sem_inc(sem, 1)


def wait_emptied(engine, s_free, bank_and_value):
    bank, value = bank_and_value
    wait(engine, s_free[bank], value)


class Iteration:

    def __init__(self, pair, odd, n_seq):
        self.pair = pair
        self.b = 2 * pair + odd
        self.odd = odd % 2
        self.known = isinstance(pair, int)
        self.n_seq = n_seq

    def on(self, offset):
        return not self.known or 0 <= self.b + offset < self.n_seq

    def rounds_before(self, b, name):
        total = 0
        for c in range(-1, b + 1):
            for n in NAMES:
                if c == b and n == name:
                    return total
                total += 0 <= c + OFFSET[n] < self.n_seq
        return total

    def number(self, name, shift=0):
        if self.known:
            return self.rounds_before(self.b + shift, name), 0
        return (len(NAMES) * (self.odd + shift - 2) + self.rounds_before(2, NAMES[0]) + NAMES.index(name),
                2 * len(NAMES))

    def full(self, name, shift=0):
        known, per_pair = self.number(name, shift)
        return self.pair * per_pair + (known + 1) if per_pair else known + 1

    def bank(self, name):
        return self.number(name)[0] % 2

    def emptied(self, name, shift=0, rounds=0):
        known, per_pair = self.number(name, shift)
        known -= rounds
        value = known // 2 + 1
        return known % 2, (self.pair * (per_pair // 2) + value if per_pair else value)


def iterations(engine, n_seq, body):
    for b in (-1, 0, 1):
        body(Iteration(b // 2, b % 2, n_seq))
    with engine.Fori(1, n_seq // 2 - 1) as pair:
        body(Iteration(pair, 0, n_seq))
        body(Iteration(pair, 1, n_seq))
    for b in range(n_seq - 2, n_seq + 2):
        body(Iteration(b // 2, b % 2, n_seq))


def attention(nc, x, w_qkv, w_proj, b_proj, w_gate, x1_dram, table):
    n_seq = x.shape[0]
    cap = table.shape[0] // EXPERTS
    n_fill = table.shape[0] // SEQ

    x_rows = x.rearrange("b (p t) c -> b p (t c)", t=TILES)
    x1_rows = x1_dram.rearrange("(b p t) c -> b p t c", p=P, t=TILES)
    table_rows = table.rearrange("(n p t) c -> n p (t c)", p=P, t=TILES)

    with ExitStack() as ctx:
        def sb(name, shape, dt=F32):
            return ctx.enter_context(nc.sbuf_tensor(name, shape, dt))

        def psum(name, shape):
            return ctx.enter_context(nc.psum_tensor(name, shape, F32))

        def sem(name):
            return ctx.enter_context(nc.semaphore(name))

        ps_rows = [psum(f"ps_rows{i}", [P, SEQ]) for i in range(ROWS)]
        ps_cols = [psum(f"ps_cols{i}", [P, SEQ]) for i in range(2)]
        ps_pv = psum("ps_pv", [P, SEQ])
        ps_round = [psum(f"ps_round{i}", [P, SEQ]) for i in range(2)]

        ident = sb("ident", [P, P])
        before = sb("before", [P, P], BF16)
        ones = sb("ones", [P, P], BF16)
        half = sb("half", [P, TILES])
        number = sb("number", [P, EXPERTS])
        w_in = sb("w_in", [P, KT, 3 * DIM])
        w_qk = sb("w_qk", [P, KT, 4, P])
        w_out = sb("w_out", [P, KT, DIM])
        bias = sb("bias", [P, DIM])
        gate_rows = sb("gate_rows", [EXPERTS, DIM])
        gate_t = sb("gate_t", [P, KT, EXPERTS])
        zero_rows = sb("zero_rows", [2 * UNITS, P])
        blank = sb("blank", [P, TILES, ROW])

        xs = sb("xs", [P, TILES, DIM])
        xb = [sb(f"xb{i}", [P, TILES, DIM]) for i in range(2)]
        x_t = sb("x_t", [P, KT, SEQ])
        qk_hi = [sb(f"qk_hi{i}", [P, 4, SEQ], F32R) for i in range(2)]
        qk_lo = [sb(f"qk_lo{i}", [P, 4, SEQ], F32R) for i in range(2)]
        v = [sb(f"v{i}", [P, TILES, HEADS, HD + 1]) for i in range(2)]
        q_stack = [sb(f"q_stack{g}", [P, HG, SEQ], F32R) for g in range(GROUPS)]
        k_stack = [sb(f"k_stack{g}", [P, HG, SEQ], F32R) for g in range(GROUPS)]
        peak = [sb(f"peak{i}", [P, UNITS]) for i in range(2)]
        peak_parts = [sb(f"peak_parts{i}", [P, 2 * UNITS], F32R) for i in range(2)]
        peak_rows = [sb(f"peak_rows{i}", [2 * UNITS, P]) for i in range(2)]
        probs = sb("probs", [P, RING, SEQ])
        pv = sb("pv", [P, SEQ])
        rsum = sb("rsum", [P, UNITS])
        o = sb("o", [P, TILES, DIM])
        o_t = sb("o_t", [P, KT, SEQ])
        y = sb("y", [P, TILES, DIM])
        stats = sb("stats", [P, TILES, 6])
        mv = sb("mv", [P, TILES, 2])
        var_eps = sb("var_eps", [P, TILES])
        rstd = sb("rstd", [P, TILES])
        row = sb("row", [P, TILES, ROW])
        x1_t = sb("x1_t", [P, KT, SEQ])
        logit_t = sb("logit_t", [EXPERTS, SEQ])
        logit = sb("logit", [P, TILES, EXPERTS])
        top = sb("top", [P, TILES, 8])
        top_i = sb("top_i", [P, TILES, 8], U32)
        chosen = sb("chosen", [P, TOPK, TILES])
        hot = sb("hot", [P, TOPK * TILES, EXPERTS])
        both = sb("both", [P, TILES, EXPERTS])
        count = sb("count", [P, TILES, EXPERTS])
        row_count = sb("row_count", [P, EXPERTS], BF16)
        carry = sb("carry", [P, EXPERTS], BF16)
        pos_all = sb("pos_all", [P, TILES, EXPERTS])
        hot_pos = sb("hot_pos", [P, TOPK * TILES, EXPERTS])
        pos = sb("pos", [P, TOPK * TILES])
        over = sb("over", [P, TOPK * TILES])
        slot_f = sb("slot_f", [P, TOPK * TILES])
        slot = sb("slot", [P, TOPK * TILES], U32)
        lead = sb("lead", [P, TILES])
        e_lead = sb("e_lead", [P, TILES])
        e_sum = sb("e_sum", [P, TILES])
        g0 = sb("g0", [P, TILES])
        token = sb("token", [P, TILES])

        s_const = sem("s_const")
        s_zero = sem("s_zero")
        s_pad = sem("s_pad")
        s_weights = sem("s_weights")
        s_wqk = sem("s_wqk")
        s_blank = sem("s_blank")
        s_gate = sem("s_gate")
        s_fill = sem("s_fill")
        s_x = sem("s_x")
        s_xb = sem("s_xb")
        s_stack = [sem(f"s_stack{g}") for g in range(GROUPS)]
        s_aug = [sem(f"s_aug{g}") for g in range(GROUPS)]
        s_rows = sem("s_rows")
        s_max = sem("s_max")
        s_phi = sem("s_phi")
        s_parts = sem("s_parts")
        s_cols = sem("s_cols")
        s_exp = sem("s_exp")
        s_pv = sem("s_pv")
        s_pvout = sem("s_pvout")
        s_full = sem("s_full")
        s_free = [sem(f"s_free{i}") for i in range(2)]
        s_hi = sem("s_hi")
        s_rsum = sem("s_rsum")
        s_bn = sem("s_bn")
        s_pool = sem("s_pool")
        s_x1 = sem("s_x1")
        s_y = sem("s_y")
        s_route = sem("s_route")
        s_lead = sem("s_lead")
        s_slot = sem("s_slot")
        s_scatter = sem("s_scatter")

        s_waited_sp, s_waited_pool = sem("s_waited_sp"), sem("s_waited_pool")
        s_waited_pe, s_waited_dve = sem("s_waited_pe"), sem("s_waited_dve")

        ROUTE = 28
        COUNTED, LED = 15, 16

        block = ctx.enter_context(nc.Block())

        @block.sync
        def _(sp):
            sp.dma_start(xs[:].rearrange("p t c -> p (t c)"), x_rows[0]).then_inc(s_x, 16)
            sp.dma_start(w_in[:], w_qkv.rearrange("(k p) n -> p k n", p=P)).then_inc(s_weights, 16)
            sp.dma_start(w_out[:], w_proj.rearrange("(k p) n -> p k n", p=P)).then_inc(s_weights, 16)
            sp.dma_start(gate_rows[:], w_gate).then_inc(s_weights, 16)
            sp.dma_start(bias[:], b_proj.rearrange("(a n) -> a n", a=1).to_broadcast([P, DIM])).then_inc(s_weights, 16)
            sp.wait_ge(s_zero, 1)
            filled = [0]

            def fill(n):
                for i in range(filled[0], min(filled[0] + n, n_fill)):
                    if i == 0:
                        sp.wait_ge(s_blank, 2)
                    sp.dma_start(table_rows[i], blank[:].rearrange("p t c -> p (t c)")).then_inc(s_fill, 16)
                filled[0] = min(filled[0] + n, n_fill)

            fill(n_fill // 10)

            def body(it):
                b = it.b
                for s in range(4):
                    g, off = (s + 1) % 4, 0 if s < 3 else 1
                    if it.on(off):
                        wait(sp, s_cols, (b + (off - 1)) * 64 + (UNITS * (g + 1)))
                        settle(sp, s_waited_sp)
                        wait_emptied(sp, s_free, it.emptied("qk3", off - 1))
                        if it.known and b + off == 0:
                            sp.wait_ge(s_pad, 3 * g + 3)
                        par = (it.odd + off) % 2
                        m, part = g // 2, slice(GP * (g % 2), GP * (g % 2) + GP)
                        hi, lo = qk_hi[par], qk_lo[par]
                        for r, (a, c) in enumerate([(hi, hi), (lo, hi), (hi, lo), (lo, lo)]):
                            rows = slice(HD * r, HD * r + HD)
                            sp.dma_start(q_stack[g][rows].bitcast(F32), a[part, m, :].bitcast(F32)).then_inc(s_stack[g], 16)
                            sp.dma_start(k_stack[g][rows].bitcast(F32), c[part, 2 + m, :].bitcast(F32)).then_inc(s_stack[g], 16)
                        sp.dma_start(q_stack[g][STACK:STACK + AUG].bitcast(F32), zero_rows[:]).then_inc(s_stack[g], 16)
                    g, off = (s - 1) % 4, 0 if s > 0 else -1
                    if it.on(off):
                        wait_emptied(sp, s_free, it.emptied(f"peak{g}"))
                        sp.dma_start(q_stack[g][STACK:STACK + AUG].bitcast(F32), peak_rows[g % 2][:]).then_inc(s_aug[g], 16)
                    if s == 0 and it.on(-2):
                        wait(sp, s_x1, (b - 1) * TILES)
                        settle(sp, s_waited_sp)
                        sp.dma_start(x1_rows[b - 2], row[:, :, 0:DIM]).then_inc(s_y, 16)
                    if s == 3 and it.on(2):
                        sp.wait_ge(s_xb, b + 2)
                        settle(sp, s_waited_sp)
                        sp.wait_ge(s_full, it.full("xT1"))
                        settle(sp, s_waited_sp)
                        sp.dma_start(xs[:].rearrange("p t c -> p (t c)"), x_rows[b + 2]).then_inc(s_x, 16)
                    if it.known and (b, s) >= (-1, 3):
                        fill(n_fill * 9 // 80)

            iterations(sp, n_seq, body)
            sp.wait_ge(s_fill, 16 * n_fill)
            sp.wait_ge(s_y, 16 * n_seq)

        @block.gpsimd
        def _(pool):
            pool.memset(ident[:], 0.0).then_inc(s_const, 1)
            pool.memset(before[:], 1.0).then_inc(s_const, 1)
            pool.memset(ones[:], 1.0).then_inc(s_const, 1)
            pool.memset(half[:], -0.5).then_inc(s_const, 1)
            pool.memset(blank[:], 0.0).then_inc(s_blank, 1)
            pool.iota(number[:], [[1, EXPERTS]], base=0, channel_multiplier=0,
                      allow_small_or_imprecise_dtypes=True).then_inc(s_const, 1)
            pool.iota(token[:], [[1, TILES]], base=0, channel_multiplier=TILES,
                      allow_small_or_imprecise_dtypes=True).then_inc(s_const, 1)
            pool.wait_ge(s_const, 6)
            pool.affine_select(out=ident[:], in_=ident[:], compare_op=ALU.not_equal, fill=1.0, base=0,
                               pattern=[[-1, P]], channel_multiplier=1).then_inc(s_const, 1)
            pool.affine_select(out=before[:], in_=before[:], compare_op=ALU.is_gt, fill=0.0, base=0,
                               pattern=[[1, P]], channel_multiplier=-1).then_inc(s_const, 1)
            pool.wait_ge(s_blank, 1)
            pool.memset(blank[:].bitcast(U32)[:, :, C_ID:C_ID + 1], FAR).then_inc(s_blank, 1)
            for g in range(GROUPS):
                if g == 0:
                    pool.wait_ge(s_blank, 2)
                else:
                    pool.wait_ge(s_pad, 3 * g)
                pool.memset(k_stack[g][STACK:].bitcast(F32), 0.0).then_inc(s_pad, 1)
                pool.wait_ge(s_pad, 3 * g + 1)
                pool.memset(k_stack[g][STACK:STACK + AUG].bitcast(F32), 1.0).then_inc(s_pad, 1)
                pool.wait_ge(s_pad, 3 * g + 2)
                pool.memset(q_stack[g][STACK:].bitcast(F32), 0.0).then_inc(s_pad, 1)
            pool.wait_ge(s_pad, 3 * GROUPS)
            pool.wait_ge(s_weights, 64)

            def body(it):
                b = it.b
                for s in range(4):
                    if s == 2 and it.on(-2):
                        pool.wait_ge(s_slot, b - 1)
                        pool.wait_ge(s_fill, 16 * n_fill)
                        settle(pool, s_waited_pool)
                        for k in range(TOPK):
                            for t in range(TILES):
                                c = k * TILES + t
                                pool.indirect_dma_start(
                                    table, bass.IndirectOffsetOnAxis(ap=slot[:, c:c + 1], axis=0), row[:, t, :], None,
                                    bounds_check=table.shape[0] - 1, oob_is_err=False).then_inc(s_scatter, 16)
                    if s == 3:
                        if it.on(-1):
                            pool.wait_ge(s_bn, 8 * b)
                            settle(pool, s_waited_pool)
                            pool.tensor_scalar(var_eps[:], mv[:, :, 1], EPS, None, ALU.add).then_inc(s_pool, 1)
                            pool.wait_ge(s_pool, 2 * b - 1)
                            pool.tensor_tensor(rstd[:], var_eps[:], half[:], ALU.pow).then_inc(s_pool, 1)
                            pool.wait_ge(s_pool, 2 * b)
                            wait(pool, s_scatter, (b - 1) * (16 * TOPK * TILES))
                            wait(pool, s_y, (b - 1) * 16)
                            settle(pool, s_waited_pool)
                            for t in range(TILES):
                                pool.tensor_scalar(row[:, t, 0:DIM], y[:, t, :], mv[:, t, 0:1], rstd[:, t:t + 1],
                                                   ALU.subtract, ALU.mult).then_inc(s_x1, 1)
                        if it.on(1):
                            pool.wait_ge(s_x, 16 * (b + 2))
                            if it.on(-1):
                                wait_emptied(pool, s_free, it.emptied("proj1"))
                            pool.tensor_tensor(xb[(it.odd + 1) % 2][:], xs[:],
                                               bias[:].rearrange("p (a c) -> p a c", a=1).to_broadcast([P, TILES, DIM]),
                                               ALU.add).then_inc(s_xb, 1)

            iterations(pool, n_seq, body)
            pool.wait_ge(s_scatter, 16 * TOPK * TILES * n_seq)

        @block.tensor
        def _(pe):
            pe.wait_ge(s_weights, 64)
            pe.wait_ge(s_const, 8)
            for k in range(KT):
                last = pe.transpose(ps_round[0][:, k * EXPERTS:(k + 1) * EXPERTS], gate_rows[:, k * P:(k + 1) * P],
                                    ident[0:EXPERTS, 0:EXPERTS])
            last.then_inc(s_gate, 1)
            pe.wait_ge(s_gate, 2)
            pe.wait_ge(s_wqk, 1)
            pe.wait_ge(s_zero, 2)

            def round_(it, name):
                b = it.b
                ps_m = ps_round[it.bank(name)]
                wait_emptied(pe, s_free, it.emptied(name, rounds=2))
                kind, n = name.rstrip("0123"), int(name[-1]) if name[-1].isdigit() else 0

                def result_of(earlier, shift=0):
                    if it.emptied(earlier, shift)[0] != it.bank(name):
                        wait_emptied(pe, s_free, it.emptied(earlier, shift))

                if kind == "peak":
                    pe.wait_ge(s_parts, (b + OFFSET[name]) * GROUPS + (n + 1))
                    last = pe.transpose(ps_m[0:2 * UNITS, 0:P], peak_parts[n % 2][:].bitcast(F32), ident[:])
                elif kind == "xT":
                    pe.wait_ge(s_x, 16 * (b + 2))
                    for t in range(TILES):
                        last = pe.transpose(ps_m[:, t * P:(t + 1) * P], xs[:, t, n * P:(n + 1) * P], ident[:])
                elif kind == "qk":
                    if n == 0:
                        result_of("xT1")
                    for k in range(KT):
                        last = pe.matmul(ps_m[:], w_qk[:, k, n, :], x_t[:, k, :], start=k == 0, stop=k == KT - 1)
                elif kind == "v":
                    for t in range(2):
                        for k in range(KT):
                            tok = slice((2 * n + t) * P, (2 * n + t + 1) * P)
                            last = pe.matmul(ps_m[:, t * DIM:(t + 1) * DIM], x_t[:, k, tok], w_in[:, k, 2 * DIM:],
                                             start=k == 0, stop=k == KT - 1)
                elif kind == "turn":
                    pe.wait_ge(s_pvout, (b + OFFSET[name]) * GROUPS + (n + 1))
                    for t in range(TILES):
                        last = pe.transpose(ps_m[:, t * P:(t + 1) * P], pv[:, t * P:(t + 1) * P], ident[:])
                elif kind == "oT":
                    if n == 0:
                        result_of("turn3")
                        settle(pe, s_waited_pe)
                    for t in range(TILES):
                        last = pe.transpose(ps_m[:, t * P:(t + 1) * P], o[:, t, n * P:(n + 1) * P], ident[:])
                elif kind == "proj":
                    if n == 0:
                        result_of("oT1")
                    for t in range(2):
                        for k in range(KT):
                            tok = slice((2 * n + t) * P, (2 * n + t + 1) * P)
                            last = pe.matmul(ps_m[:, t * DIM:(t + 1) * DIM], o_t[:, k, tok], w_out[:, k, :],
                                             start=k == 0, stop=k == KT - 1)
                elif kind == "x1T":
                    pe.wait_ge(s_x1, (b - 1) * TILES)
                    for t in range(TILES):
                        last = pe.transpose(ps_m[:, t * P:(t + 1) * P], row[:, t, n * P:(n + 1) * P], ident[:])
                elif kind == "logit":
                    result_of("x1T1")
                    for k in range(KT):
                        last = pe.matmul(ps_m[0:EXPERTS, :], gate_t[:, k, :], x1_t[:, k, :], start=k == 0,
                                         stop=k == KT - 1)
                elif kind == "logitT":
                    result_of("logit")
                    settle(pe, s_waited_pe)
                    for t in range(TILES):
                        last = pe.transpose(ps_m[:, t * EXPERTS:(t + 1) * EXPERTS], logit_t[:, t * P:(t + 1) * P],
                                            ident[0:EXPERTS, 0:EXPERTS])
                else:
                    pe.wait_ge(s_route, (b - 2) * ROUTE + COUNTED)
                    pe.matmul(ps_m[:, 0:EXPERTS], before[:], row_count[:], start=True, stop=False)
                    last = pe.matmul(ps_m[:, 0:EXPERTS], ones[:], carry[:], start=False, stop=True)
                last.then_inc(s_full, 1)

            def body(it):
                b = it.b
                for s in range(4):
                    for j in range(UNITS):
                        if it.on(0):
                            if j == 0:
                                pe.wait_ge(s_stack[s], (b + 1) * (16 * 9))
                            n = s * UNITS + j
                            last_use = n - ROWS if n >= ROWS else (ALL - 1 - (ALL - 1 - n) % ROWS) - ALL
                            wait(pe, s_max, b * ALL + (last_use + 1))
                            t, h = j % TILES, j // TILES
                            pe.matmul(ps_rows[n % ROWS][:], q_stack[s][:, h, t * P:(t + 1) * P],
                                      k_stack[s][:, h, :], start=True, stop=True).then_inc(s_rows, 1)
                        g, off = (s + 2) % 4, -1 if s < 2 else 0
                        if it.on(off):
                            if j == 0:
                                pe.wait_ge(s_aug[g], (b + (off + 1)) * 16)
                            wait(pe, s_exp, (b + off) * 64 + (16 * g + j - 1))
                            t, h = j // HG, j % HG
                            pe.matmul(ps_cols[j % 2][:], k_stack[g][:, h, t * P:(t + 1) * P], q_stack[g][:, h, :],
                                      start=True, stop=True).then_inc(s_cols, 1)
                        if j % HG == 1:
                            t = j // HG - 1
                            g, off = ((s + 2) % 4, -1 if s < 2 else 0) if t >= 0 else ((s + 1) % 4, -1 if s < 3 else 0)
                            t %= TILES
                            if it.on(off):
                                if t == 0:
                                    wait(pe, s_pvout, (b + off) * GROUPS + g)
                                pe.wait_ge(s_exp, (b + off) * 64 + (16 * g + HG * (t + 1)))
                                par = (it.odd + off) % 2
                                for h in range(HG):
                                    last = pe.matmul(ps_pv[32 * h:32 * h + HD + 1, :], v[par][:, t, HG * g + h, :],
                                                     probs[:, (HG * t + h) % RING, :], start=t == 0, stop=t == TILES - 1)
                                last.then_inc(s_pv, 1)
                        name = AT.get((s, j))
                        if name and it.on(OFFSET[name]):
                            round_(it, name)

            iterations(pe, n_seq, body)

        @block.scalar
        def _(act):
            def body(it):
                b = it.b

                def full(name):
                    act.wait_ge(s_full, it.full(name))

                def copy_out(name, out, in_):
                    full(name)
                    act.copy(out, in_).then_inc(s_free[it.bank(name)], 1)

                def empty(s, j):
                    name = AT.get((s, j))
                    if name and it.on(OFFSET[name]):
                        ps_m = ps_round[it.bank(name)]
                        kind, n = name.rstrip("0123"), int(name[-1]) if name[-1].isdigit() else 0
                        if kind == "peak":
                            beta = b + OFFSET[name]
                            if n >= 2:
                                act.wait_ge(s_aug[n - 2], (beta + 1) * 16)
                            else:
                                wait(act, s_aug[n + 2], beta * 16)
                            copy_out(name, peak_rows[n % 2][:], ps_m[0:2 * UNITS, 0:P])
                        elif kind == "xT":
                            copy_out(name, x_t[:, n, :], ps_m[:])
                        elif kind == "qk":
                            full(name)
                            act.copy(qk_hi[(it.odd + 1) % 2][:, n, :], ps_m[:]).then_inc(s_hi, 1)
                        elif kind == "v":
                            copy_out(name, v[(it.odd + 1) % 2][:, 2 * n:2 * n + 2, :, 0:HD],
                                     ps_m[:].rearrange("p (t h d) -> p t h d", t=2, h=HEADS))
                        elif kind == "oT":
                            copy_out(name, o_t[:, n, :], ps_m[:])
                        elif kind == "x1T":
                            copy_out(name, x1_t[:, n, :], ps_m[:])
                        elif kind == "logit":
                            copy_out(name, logit_t[:], ps_m[0:EXPERTS, :])

                for s in range(4):
                    for j in range(UNITS):
                        if j == 2:
                            g, off = (s + 1) % 4, -1 if s < 3 else 0
                            if it.on(off):
                                act.wait_ge(s_pv, (b + off) * 16 + (4 * g + 4))
                                before_ = {0: ("turn0", -1), 1: ("turn1", 0), 2: ("turn2", 0), 3: ("turn3", 0)}[s]
                                if not it.known or (it.b + off) * 4 + g > 0:
                                    act.wait_ge(s_full, it.full(*before_))
                                act.copy(pv[:], ps_pv[:]).then_inc(s_pvout, 1)
                        if j:
                            empty(s, j - 1)
                        g, off = (s + 2) % 4, -1 if s < 2 else 0
                        if it.on(off):
                            if j % HG == 0:
                                wait(act, s_pv, (b + off) * 16 + (4 * g + j // HG - 1))
                            act.wait_ge(s_cols, (b + off) * 64 + (16 * g + j + 1))
                            act.activation(probs[:, j % RING, :], ps_cols[j % 2][:], ACT.Exp,
                                           scale=SCALE).then_inc(s_exp, 1)
                        if j == UNITS - 1:
                            empty(s, j)
                        if s == 1 and j == 14 and it.on(-2):
                            act.wait_ge(s_route, (b - 2) * ROUTE + LED)
                            act.activation(e_lead[:], lead[:], ACT.Exp).then_inc(s_lead, 1)

            iterations(act, n_seq, body)

        @block.vector
        def _(dve):
            dve.memset(zero_rows[:], 0.0).then_inc(s_zero, 1)
            dve.wait_ge(s_weights, 64)
            for m in range(4):
                for g in range(2):
                    src = w_in[:, :, m * P + g * GP:m * P + (g + 1) * GP].rearrange("p k (h r) -> p k r h", h=HG)
                    for k in range(KT):
                        last = dve.tensor_copy(w_qk[:, k, m, g * GP:(g + 1) * GP].rearrange("p (r h) -> p r h", h=HG),
                                               src[:, k])
            last.then_inc(s_wqk, 1)
            dve.wait_ge(s_gate, 1)
            dve.tensor_copy(gate_t[:].rearrange("p k e -> p (k e)"), ps_round[0][:, 0:KT * EXPERTS]).then_inc(s_gate, 1)
            for i in range(2):
                dve.memset(v[i][:, :, :, HD:HD + 1], 1.0)
            dve.memset(ps_pv[:], 0.0)
            dve.memset(carry[:], 0.0)
            dve.memset(count[:, 0, :], 0.0).then_inc(s_zero, 1)

            def body(it):
                b = it.b

                def full(name):
                    dve.wait_ge(s_full, it.full(name))

                def turn_sums(name, g):
                    full(name)
                    ps_m = ps_round[it.bank(name)]
                    parts = ps_m[:].rearrange("p (u d) -> p u d", d=32)
                    dve.reciprocal(rsum[:], parts[:, :, HD]).then_inc(s_rsum, 1)

                def turn(name, g):
                    beta = b + OFFSET[name]
                    ps_m = ps_round[it.bank(name)]
                    dve.wait_ge(s_rsum, beta * GROUPS + (g + 1))
                    dve.tensor_tensor(
                        o[:, :, g * GP:(g + 1) * GP].rearrange("p t (h d) -> p t h d", h=HG),
                        ps_m[:].rearrange("p (t h d) -> p t h d", t=TILES, h=HG)[:, :, :, 0:HD],
                        rsum[:].rearrange("p (t h a) -> p t h a", t=TILES, a=1).to_broadcast([P, TILES, HG, HD]),
                        ALU.mult).then_inc(s_free[it.bank(name)], 1)

                def low_part(n):
                    par = (it.odd + 1) % 2
                    dve.wait_ge(s_hi, (b + 1) * 4 + (n + 1))
                    bank = it.bank(f"qk{n}")
                    dve.tensor_tensor(qk_lo[par][:, n, :], ps_round[bank][:], qk_hi[par][:, n, :].bitcast(F32),
                                      ALU.subtract).then_inc(s_free[bank], 1)

                def project(n):
                    beta = b - 1
                    full(f"proj{n}")
                    bank = it.bank(f"proj{n}")
                    tt = slice(2 * n, 2 * n + 2)
                    if n == 0:
                        wait(dve, s_x1, beta * TILES)
                    dve.tensor_tensor(y[:, tt, :], ps_round[bank][:].rearrange("p (t c) -> p t c", t=2),
                                      xb[(it.odd + 1) % 2][:, tt, :], ALU.add).then_inc(s_free[bank], 1)
                    wait_emptied(dve, s_free, it.emptied(f"proj{n}"))
                    for t in (2 * n, 2 * n + 1):
                        dve.bn_stats(stats[:, t, :], y[:, t, :]).then_inc(s_bn, 1)
                    for t in (2 * n, 2 * n + 1):
                        dve.wait_ge(s_bn, beta * 8 + (4 * n + t - 2 * n + 1))
                        settle(dve, s_waited_dve)
                        dve.bn_aggr(mv[:, t, :], stats[:, t, :]).then_inc(s_bn, 1)

                link_no = [0]

                def link(ins):
                    link_no[0] += 1
                    ins.then_inc(s_route, 1)
                    dve.wait_ge(s_route, (b - 2) * ROUTE + link_no[0])

                def route_top():
                    full("logitT")
                    bank = it.bank("logitT")
                    dve.tensor_copy(logit[:].rearrange("p t e -> p (t e)"),
                                    ps_round[bank][:, 0:TILES * EXPERTS]).then_inc(s_free[bank], 1)
                    wait_emptied(dve, s_free, it.emptied("logitT"))
                    settle(dve, s_waited_dve)
                    for t in range(TILES):
                        last = dve.max(top[:, t, :], logit[:, t, :])
                        if t < TILES - 1:
                            last.then_inc(s_route, 1)
                            link_no[0] += 1
                    link(last)

                def route_experts():
                    settle(dve, s_waited_dve)
                    for t in range(TILES):
                        last = dve.max_index(top_i[:, t, :], top[:, t, :], logit[:, t, :])
                        if t < TILES - 1:
                            last.then_inc(s_route, 1)
                            link_no[0] += 1
                    link(last)

                def route_hot():
                    link(dve.tensor_copy(chosen[:], top_i[:, :, 0:TOPK].rearrange("p t k -> p k t")))
                    link(dve.tensor_tensor(
                        hot[:], number[:].rearrange("p (a e) -> p a e", a=1).to_broadcast([P, TOPK * TILES, EXPERTS]),
                        chosen[:].rearrange("p k (t a) -> p (k t) a", a=1).to_broadcast([P, TOPK * TILES, EXPERTS]),
                        ALU.is_equal))
                    link(dve.tensor_tensor(both[:], hot[:, 0:TILES, :], hot[:, TILES:, :], ALU.add))

                def route_count():
                    for t in range(1, TILES):
                        link(dve.tensor_tensor(count[:, t, :], count[:, t - 1, :], both[:, t - 1, :], ALU.add))
                    link(dve.tensor_tensor(row_count[:], count[:, TILES - 1, :], both[:, TILES - 1, :], ALU.add))
                    link(dve.tensor_tensor(lead[:], top[:, :, 1], top[:, :, 0], ALU.subtract))

                def route_place():
                    full("place")
                    bank = it.bank("place")
                    base = ps_round[bank][:, 0:EXPERTS].rearrange("p (a e) -> p a e", a=1).to_broadcast([P, TILES, EXPERTS])
                    dve.tensor_tensor(pos_all[:], count[:], base, ALU.add).then_inc(s_free[bank], 1)
                    wait_emptied(dve, s_free, it.emptied("place"))
                    link(dve.tensor_tensor(carry[:], carry[:], row_count[:], ALU.add))
                    for k in range(TOPK):
                        link(dve.tensor_tensor(hot_pos[:, k * TILES:(k + 1) * TILES, :],
                                               hot[:, k * TILES:(k + 1) * TILES, :], pos_all[:], ALU.mult))

                def route_slots():
                    link(dve.tensor_reduce(pos[:], hot_pos[:], AX.X, ALU.add))
                    link(dve.tensor_scalar(over[:], pos[:], float(cap), float(FAR), ALU.is_ge, ALU.mult))
                    link(dve.scalar_tensor_tensor(slot_f[:], chosen[:].rearrange("p k t -> p (k t)"), float(cap),
                                                  pos[:], ALU.mult, ALU.add))
                    wait(dve, s_scatter, (b - 2) * (16 * TOPK * TILES))
                    link(dve.tensor_tensor(slot[:], slot_f[:], over[:], ALU.add))

                def route_gates():
                    dve.wait_ge(s_lead, b - 1)
                    link(dve.tensor_scalar(e_sum[:], e_lead[:], 1.0, None, ALU.add))
                    link(dve.reciprocal(g0[:], e_sum[:]))
                    link(dve.tensor_tensor(row[:, :, C_G1], e_lead[:], g0[:], ALU.mult))
                    link(dve.tensor_tensor(row[:, :, C_DIFF], g0[:], row[:, :, C_G1], ALU.subtract))
                    dve.tensor_copy(row[:, :, C_E0], chosen[:, 0, :])
                    link(dve.tensor_copy(row[:].bitcast(U32)[:, :, C_ID], token[:]))
                    dve.tensor_scalar(token[:], token[:], float(SEQ), None, ALU.add).then_inc(s_slot, 1)

                route = {(1, 0): route_top, (1, 3): route_experts, (1, 4): route_hot, (1, 7): route_count,
                         (1, 15): route_place, (2, 0): route_slots, (2, 4): route_gates}
                for s in range(4):
                    for j in range(UNITS):
                        if (s, j) in route and it.on(-2):
                            route[s, j]()
                        if it.on(0):
                            n = s * UNITS + j
                            dve.wait_ge(s_rows, b * ALL + (n + 1))
                            if j == 0:
                                wait(dve, s_parts, b * GROUPS + (s - 1))
                            dve.tensor_reduce(peak[s % 2][:, j:j + 1], ps_rows[n % ROWS][:], AX.X, ALU.max,
                                              negate=True).then_inc(s_max, 1)
                        g, off = (s - 1) % 4, 0 if s > 0 else -1
                        if j in (1, 2) and it.on(off):
                            parts = peak_parts[g % 2]
                            if j == 1:
                                if not it.known or (b + off, g) >= (0, 2):
                                    dve.wait_ge(s_full, it.full(f"peak{(g - 2) % 4}", -1 if g in (0, 3) else 0))
                                dve.wait_ge(s_max, b * ALL + s * UNITS)
                                dve.tensor_copy(parts[:, 0:UNITS], peak[g % 2][:]).then_inc(s_phi, 1)
                            else:
                                dve.wait_ge(s_phi, b * GROUPS + s)
                                dve.tensor_tensor(parts[:, UNITS:], peak[g % 2][:], parts[:, 0:UNITS].bitcast(F32),
                                                  ALU.subtract).then_inc(s_parts, 1)
                        if j in (8, 9) and it.on(-1 if s < 3 else 0):
                            (turn_sums if j == 8 else turn)(f"turn{(s + 1) % 4}", (s + 1) % 4)
                        low = {(1, 5): 0, (1, 13): 1, (2, 0): 2, (2, 5): 3}
                        if it.on(1) and (s, j) in low:
                            low_part(low[s, j])
                        if s == 3 and j == 0 and it.on(-1):
                            project(0)
                        if s == 3 and j == 5 and it.on(-1):
                            project(1)

            iterations(dve, n_seq, body)


def experts(nc, table, w1, w2, x1_dram):
    cap = table.shape[0] // EXPERTS
    per = cap // SEQ
    n_chunks = EXPERTS * per
    n_tokens = x1_dram.shape[0]
    assert cap % SEQ == 0 and per % 2 == 0 and EXPERTS % 2 == 0 and EXPERTS > 4 and per > 2
    chunk_rows = table.rearrange("(n p t) c -> n p (t c)", p=P, t=TILES)
    w1_rows = w1.rearrange("e (k p) f -> e p k f", p=P)
    w2_rows = w2.rearrange("e (k p) d -> e p k d", p=P)

    with ExitStack() as ctx:
        def sb(name, shape, dt=F32):
            return ctx.enter_context(nc.sbuf_tensor(name, shape, dt))

        def psum(name, shape):
            return ctx.enter_context(nc.psum_tensor(name, shape, F32))

        def sem(name):
            return ctx.enter_context(nc.semaphore(name))

        ps_turn = [psum(f"ps_turn{i}", [P, SEQ]) for i in range(KT)]
        ps_hid = [psum(f"ps_hid{i}", [P, 2, SEQ]) for i in range(2)]
        ps_out = psum("ps_out", [P, TILES, DIM])

        ident = sb("ident_e", [P, P])
        rows = [sb(f"rows{i}", [P, TILES, ROW]) for i in range(2)]
        x_hi = [sb(f"x_hi{i}", [P, KT, SEQ], F32R) for i in range(2)]
        x_lo = [sb(f"x_lo{i}", [P, KT, SEQ], F32R) for i in range(2)]
        raw1 = sb("raw1", [P, KT, 2 * FF])
        raw2 = sb("raw2", [P, FT, DIM])
        w1_hi = [sb(f"w1_hi{i}", [P, KT, 2 * FF], F32R) for i in range(2)]
        w1_lo = [sb(f"w1_lo{i}", [P, KT, 2 * FF], F32R) for i in range(2)]
        w2_hi = [sb(f"w2_hi{i}", [P, FT, DIM], F32R) for i in range(2)]
        w2_lo = [sb(f"w2_lo{i}", [P, FT, DIM], F32R) for i in range(2)]
        act_in = [sb(f"act_in{i}", [P, SEQ]) for i in range(2)]
        hid = [sb(f"hid{i}", [P, SEQ]) for i in range(2)]
        h_hi = [sb(f"h_hi{i}", [P, FT, SEQ], F32R) for i in range(2)]
        h_lo = [sb(f"h_lo{i}", [P, FT, SEQ], F32R) for i in range(2)]
        out = [sb(f"out{i}", [P, TILES, DIM]) for i in range(2)]
        gate = [sb(f"gate{i}", [P, TILES]) for i in range(2)]
        gate_part = sb("gate_part", [P, TILES])
        token = [sb(f"token{i}", [P, TILES], U32) for i in range(2)]
        expert_no = sb("expert_no", [P, 1])

        s_ident = sem("s_ident")
        s_rows = [sem(f"s_rows{i}") for i in range(2)]
        s_raw = sem("s_raw")
        s_whi = sem("s_whi")
        s_w = sem("s_w")
        s_turn = sem("s_turn")
        s_xhi = sem("s_xhi")
        s_xlo = sem("s_xlo")
        s_hid = sem("s_hid")
        s_gelu = sem("s_gelu")
        s_mul = sem("s_mul")
        s_hhi = sem("s_hhi")
        s_hlo = sem("s_hlo")
        s_out = sem("s_out")
        s_gp = sem("s_gp")
        s_meta = sem("s_meta")
        s_scaled = sem("s_scaled")
        s_add = sem("s_add")
        s_eno = sem("s_eno")

        s_waited_sp, s_waited_pool = sem("s_waited_sp_e"), sem("s_waited_pool_e")

        W_PIECES = 3
        ADDED = 16 * TILES

        class Chunk:

            def __init__(self, e, par, lead, half, odd, last=False):
                self.e, self.par, self.lead, self.half, self.odd, self.last = e, par, lead, half, odd, last
                self.n = half * 2 + odd
                self.first = isinstance(half, int) and self.n == 0
                self.final_expert = isinstance(e, int) and e == EXPERTS - 1

        def chunks(engine, body):
            halves = per // 2

            def expert(e, par, final=False):
                for odd in range(2):
                    body(Chunk(e, par, True, e * halves, odd))
                with engine.Fori(1, halves - 1 if final else halves) as i:
                    for odd in range(2):
                        body(Chunk(e, par, False, e * halves + i, odd))
                if final:
                    for odd in range(2):
                        body(Chunk(e, par, False, e * halves + halves - 1, odd, last=True))

            expert(0, 0)
            expert(1, 1)
            with engine.Fori(1, EXPERTS // 2 - 1) as pair:
                expert(pair * 2, 0)
                expert(pair * 2 + 1, 1)
            expert(EXPERTS - 2, 0)
            expert(EXPERTS - 1, 1, final=True)

        def pieces(par):
            return [(raw1[:, 0], w1_hi[par][:, 0], w1_lo[par][:, 0]), (raw1[:, 1], w1_hi[par][:, 1], w1_lo[par][:, 1]),
                    (raw2[:], w2_hi[par][:], w2_lo[par][:])]

        block = ctx.enter_context(nc.Block())

        @block.sync
        def _(sp):
            def load_rows(odd, n):
                sp.dma_start(rows[odd][:].rearrange("p t c -> p (t c)"), chunk_rows[n]).then_inc(s_rows[odd], 16)

            def load_weights(e):
                sp.dma_start(raw1[:], w1_rows[e]).then_inc(s_raw, 16)
                sp.dma_start(raw2[:], w2_rows[e]).then_inc(s_raw, 16)

            load_rows(0, 0)
            load_weights(0)
            load_rows(1, 1)

            def body(k):
                if k.lead and k.odd and not k.final_expert:
                    sp.wait_ge(s_w, k.e * W_PIECES + W_PIECES)
                    settle(sp, s_waited_sp)
                    load_weights(k.e + 1)
                if not k.last:
                    sp.wait_ge(s_turn, k.n * KT + KT)
                    settle(sp, s_waited_sp)
                    sp.wait_ge(s_meta, k.n + 1)
                    settle(sp, s_waited_sp)
                    load_rows(k.odd, k.n + 2)

            chunks(sp, body)
            sp.wait_ge(s_add, n_chunks * ADDED)

        @block.gpsimd
        def _(pool):
            pool.memset(ident[:], 0.0).then_inc(s_ident, 1)
            pool.wait_ge(s_ident, 1)
            pool.affine_select(out=ident[:], in_=ident[:], compare_op=ALU.not_equal, fill=1.0, base=0,
                               pattern=[[-1, P]], channel_multiplier=1).then_inc(s_ident, 1)

            def add_out(buf, n):
                pool.wait_ge(s_scaled, n * TILES + TILES)
                wait(pool, s_add, n * ADDED)
                settle(pool, s_waited_pool)
                for t in range(TILES):
                    pool.indirect_dma_start(
                        x1_dram, bass.IndirectOffsetOnAxis(ap=token[buf][:, t:t + 1], axis=0), out[buf][:, t, :], None,
                        bounds_check=n_tokens - 1, oob_is_err=False, compute_op=ALU.add).then_inc(s_add, 16)

            def body(k):
                if not k.first:
                    add_out(1 - k.odd, k.n - 1)
                if k.lead and k.odd and not k.final_expert:
                    pool.wait_ge(s_raw, k.e * 32 + 64)
                    wait(pool, s_out, k.e * per)
                    settle(pool, s_waited_pool)
                    for i, (raw, hi, lo) in enumerate(pieces(1 - k.par)):
                        pool.tensor_copy(hi, raw).then_inc(s_whi, 1)
                        pool.wait_ge(s_whi, k.e * W_PIECES + (W_PIECES + i + 1))
                        pool.tensor_tensor(lo, raw, hi.bitcast(F32), ALU.subtract).then_inc(s_w, 1)

            chunks(pool, body)
            add_out((n_chunks - 1) % 2, n_chunks - 1)

        @block.tensor
        def _(pe):
            def turn(buf, n):
                for k in range(KT):
                    wait(pe, s_xlo, n * KT + (k + 1 - KT))
                    for t in range(TILES):
                        last = pe.transpose(ps_turn[k][:, t * P:(t + 1) * P], rows[buf][:, t, k * P:(k + 1) * P],
                                            ident[:])
                    last.then_inc(s_turn, 1)

            def hidden(c, f):
                wait(pe, s_mul, c.n * FT + (f - 1))
                for part in range(2):
                    cols = slice(part * FF + f * P, part * FF + (f + 1) * P)
                    i = 0
                    for k in range(KT):
                        for w, xx in ((w1_hi, x_hi), (w1_lo, x_hi), (w1_hi, x_lo)):
                            last = pe.matmul(ps_hid[f % 2][:, part, :], w[c.par][:, k, cols], xx[c.odd][:, k, :],
                                             start=i == 0, stop=i == 3 * KT - 1)
                            i += 1
                last.then_inc(s_hid, 1)

            def output(par, buf, n):
                wait(pe, s_scaled, n * TILES)
                pe.wait_ge(s_hlo, n * FT + FT)
                for t in range(TILES):
                    i = 0
                    for f in range(FT):
                        for hh, w in ((h_hi, w2_hi), (h_hi, w2_lo), (h_lo, w2_hi)):
                            last = pe.matmul(ps_out[:, t, :], hh[buf][:, f, t * P:(t + 1) * P], w[par][:, f, :],
                                             start=i == 0, stop=i == 3 * FT - 1)
                            i += 1
                last.then_inc(s_out, 1)

            pe.wait_ge(s_ident, 2)
            pe.wait_ge(s_rows[0], 16)
            turn(0, 0)

            def body(k):
                if not (k.last and k.odd):
                    pe.wait_ge(s_rows[1 - k.odd], (k.half + (k.odd + 1)) * 16)
                    turn(1 - k.odd, k.n + 1)
                if k.lead and not k.odd:
                    pe.wait_ge(s_w, k.e * W_PIECES + W_PIECES)
                pe.wait_ge(s_xlo, k.n * KT + KT)
                hidden(k, 0)
                hidden(k, 1)
                if not k.first:
                    output(1 - k.par if k.lead and not k.odd else k.par, 1 - k.odd, k.n - 1)
                hidden(k, 2)
                hidden(k, 3)

            chunks(pe, body)
            output(1, (n_chunks - 1) % 2, n_chunks - 1)

        @block.scalar
        def _(act):
            for i, (raw, hi, _) in enumerate(pieces(0)):
                act.wait_ge(s_raw, 32)
                act.copy(hi, raw).then_inc(s_whi, 1)

            def high_x(buf, n):
                for k in range(KT):
                    act.wait_ge(s_turn, n * KT + (k + 1))
                    act.copy(x_hi[buf][:, k, :], ps_turn[k][:]).then_inc(s_xhi, 1)

            def gelu(c, f):
                act.wait_ge(s_hid, c.n * FT + (f + 1))
                act.activation(act_in[f % 2][:], ps_hid[f % 2][:, 0, :], ACT.Gelu).then_inc(s_gelu, 1)

            def high_h(c, f):
                if f == 0:
                    wait(act, s_out, c.n - 1)
                act.wait_ge(s_mul, c.n * FT + (f + 1))
                act.copy(h_hi[c.odd][:, f, :], hid[f % 2][:]).then_inc(s_hhi, 1)

            def scale(buf, n):
                act.wait_ge(s_out, n + 1)
                act.wait_ge(s_meta, n + 1)
                wait(act, s_add, n * ADDED - ADDED)
                for t in range(TILES):
                    act.activation(out[buf][:, t, :], ps_out[:, t, :], ACT.Copy,
                                   scale=gate[buf][:, t:t + 1]).then_inc(s_scaled, 1)

            high_x(0, 0)

            def body(k):
                if not (k.last and k.odd):
                    high_x(1 - k.odd, k.n + 1)
                gelu(k, 0)
                gelu(k, 1)
                high_h(k, 0)
                high_h(k, 1)
                if not k.first:
                    scale(1 - k.odd, k.n - 1)
                gelu(k, 2)
                gelu(k, 3)
                high_h(k, 2)
                high_h(k, 3)

            chunks(act, body)
            scale((n_chunks - 1) % 2, n_chunks - 1)

        @block.vector
        def _(dve):
            dve.memset(expert_no[:], -1.0).then_inc(s_eno, 1)
            for i, (raw, hi, lo) in enumerate(pieces(0)):
                dve.wait_ge(s_whi, i + 1)
                dve.tensor_tensor(lo, raw, hi.bitcast(F32), ALU.subtract).then_inc(s_w, 1)

            def low_x(buf, n):
                for k in range(KT):
                    dve.wait_ge(s_xhi, n * KT + (k + 1))
                    dve.tensor_tensor(x_lo[buf][:, k, :], ps_turn[k][:], x_hi[buf][:, k, :].bitcast(F32),
                                      ALU.subtract).then_inc(s_xlo, 1)

            def product(c, f):
                dve.wait_ge(s_gelu, c.n * FT + (f + 1))
                wait(dve, s_hlo, c.n * FT + (f - 1))
                dve.tensor_tensor(hid[f % 2][:], ps_hid[f % 2][:, 1, :], act_in[f % 2][:],
                                  ALU.mult).then_inc(s_mul, 1)

            def low_h(c, f):
                dve.wait_ge(s_hhi, c.n * FT + (f + 1))
                dve.tensor_tensor(h_lo[c.odd][:, f, :], hid[f % 2][:], h_hi[c.odd][:, f, :].bitcast(F32),
                                  ALU.subtract).then_inc(s_hlo, 1)

            def meta(c):
                if c.lead and not c.odd:
                    dve.wait_ge(s_eno, c.e + 1)
                    dve.tensor_scalar(expert_no[:], expert_no[:], 1.0, None, ALU.add).then_inc(s_eno, 1)
                dve.wait_ge(s_eno, c.e + 2)
                wait(dve, s_scaled, c.n * TILES - TILES)
                wait(dve, s_add, c.n * ADDED - ADDED)
                r = rows[c.odd]
                dve.scalar_tensor_tensor(gate_part[:], r[:, :, C_E0], expert_no[:, 0:1], r[:, :, C_DIFF],
                                         ALU.is_equal, ALU.mult).then_inc(s_gp, 1)
                dve.wait_ge(s_gp, c.n + 1)
                dve.tensor_tensor(gate[c.odd][:], gate_part[:], r[:, :, C_G1], ALU.add)
                dve.tensor_copy(token[c.odd][:], r[:].bitcast(U32)[:, :, C_ID]).then_inc(s_meta, 1)

            low_x(0, 0)

            def body(k):
                if not (k.last and k.odd):
                    low_x(1 - k.odd, k.n + 1)
                product(k, 0)
                product(k, 1)
                low_h(k, 0)
                low_h(k, 1)
                dve.wait_ge(s_rows[k.odd], (k.half + 1) * 16)
                meta(k)
                product(k, 2)
                product(k, 3)
                low_h(k, 2)
                low_h(k, 3)

            chunks(dve, body)


def final_norm(nc, y_dram, out_dram):
    RING_Y = 4
    n_chunks = y_dram.shape[0] // SEQ
    y_rows = y_dram.rearrange("(n p t) c -> n p (t c)", p=P, t=TILES)
    out_rows = out_dram.rearrange("(n p t) c -> n p (t c)", p=P, t=TILES)
    with ExitStack() as ctx:
        def sb(name, shape, dt=F32):
            return ctx.enter_context(nc.sbuf_tensor(name, shape, dt))

        def sem(name):
            return ctx.enter_context(nc.semaphore(name))

        y = [sb(f"fy{i}", [P, TILES, DIM]) for i in range(RING_Y)]
        z = [sb(f"fz{i}", [P, TILES, DIM]) for i in range(RING_Y)]
        stats = [sb(f"fstats{i}", [P, TILES, 6]) for i in range(RING_Y)]
        mv = [sb(f"fmv{i}", [P, TILES, 2]) for i in range(RING_Y)]
        var_eps = [sb(f"fvar{i}", [P, TILES]) for i in range(RING_Y)]
        rstd = [sb(f"frstd{i}", [P, TILES]) for i in range(RING_Y)]
        half = sb("fhalf", [P, TILES])
        s_in = [sem(f"s_in{i}") for i in range(RING_Y)]
        s_store = [sem(f"s_store{i}") for i in range(RING_Y)]
        s_half = sem("s_fhalf")
        s_bn = sem("s_fbn")
        s_eps = sem("s_feps")
        s_rstd = sem("s_frstd")
        s_norm = sem("s_fnorm")

        s_waited_sp, s_waited_act = sem("s_waited_sp_f"), sem("s_waited_act_f")
        s_waited_pool, s_waited_dve = sem("s_waited_pool_f"), sem("s_waited_dve_f")

        def rings(engine, body):
            for r in range(RING_Y):
                body(r, r, 0)
            with engine.Fori(1, n_chunks // RING_Y) as q:
                for r in range(RING_Y):
                    body(q * RING_Y + r, r, q)

        block = ctx.enter_context(nc.Block())

        @block.sync
        def _(sp):
            def body(i, r, q):
                wait(sp, s_norm, i * TILES - (RING_Y - 1) * TILES)
                if not isinstance(i, int):
                    settle(sp, s_waited_sp)
                sp.dma_start(y[r][:].rearrange("p t c -> p (t c)"), y_rows[i]).then_inc(s_in[r], 16)

            rings(sp, body)

        @block.scalar
        def _(act):
            def body(i, r, q):
                act.wait_ge(s_norm, i * TILES + TILES)
                settle(act, s_waited_act)
                act.dma_start(out_rows[i], z[r][:].rearrange("p t c -> p (t c)")).then_inc(s_store[r], 16)

            rings(act, body)
            for r in range(RING_Y):
                act.wait_ge(s_store[r], 16 * (n_chunks // RING_Y))

        @block.gpsimd
        def _(pool):
            pool.memset(half[:], -0.5).then_inc(s_half, 1)
            pool.wait_ge(s_half, 1)

            def body(i, r, q):
                pool.wait_ge(s_bn, i * 8 + 8)
                wait(pool, s_norm, i * TILES - (RING_Y - 1) * TILES)
                settle(pool, s_waited_pool)
                pool.tensor_scalar(var_eps[r][:], mv[r][:, :, 1], EPS, None, ALU.add).then_inc(s_eps, 1)
                pool.wait_ge(s_eps, i + 1)
                pool.tensor_tensor(rstd[r][:], var_eps[r][:], half[:], ALU.pow).then_inc(s_rstd, 1)

            rings(pool, body)

        @block.vector
        def _(dve):
            def statistics(i, r, q):
                dve.wait_ge(s_in[r], q * 16 + 16)
                for t in range(TILES):
                    dve.bn_stats(stats[r][:, t, :], y[r][:, t, :]).then_inc(s_bn, 1)
                for t in range(TILES):
                    dve.wait_ge(s_bn, i * 8 + (t + 1))
                    settle(dve, s_waited_dve)
                    dve.bn_aggr(mv[r][:, t, :], stats[r][:, t, :]).then_inc(s_bn, 1)

            def normalise(i, r, q):
                dve.wait_ge(s_rstd, i + 1)
                wait(dve, s_store[r], q * 16)
                for t in range(TILES):
                    dve.tensor_scalar(z[r][:, t, :], y[r][:, t, :], mv[r][:, t, 0:1], rstd[r][:, t:t + 1],
                                      ALU.subtract, ALU.mult).then_inc(s_norm, 1)

            def body(i, r, q):
                statistics(i, r, q)
                if isinstance(q, int):
                    if r:
                        normalise(i - 1, r - 1, 0)
                elif r:
                    normalise(i - 1, r - 1, q)
                else:
                    normalise(i - 1, RING_Y - 1, q - 1)

            rings(dve, body)
            normalise(n_chunks - 1, RING_Y - 1, n_chunks // RING_Y - 1)


def transformer_layer(nc, x, w_qkv, w_proj, b_proj, w_gate, w1, w2, out):
    n_tokens = x.shape[0] * x.shape[1]
    cap = n_tokens * TOPK * 5 // 4 // EXPERTS
    x1 = nc.dram_tensor("x1", [n_tokens, DIM], F32).ap()
    table = nc.dram_tensor("expert_rows", [EXPERTS * cap, ROW], F32).ap()
    attention(nc, x, w_qkv, w_proj, b_proj, w_gate, x1, table)
    experts(nc, table, w1, w2, x1)
    final_norm(nc, x1, out.rearrange("b s c -> (b s) c"))


_INS = ["L0_attn_x", "L0_attn_w_qkv", "L0_attn_w_proj", "L0_attn_b_proj", "L0_ffn_Wg", "L0_ffn_W1", "L0_ffn_W2"]


def kernel(**inputs):
    import concourse.bacc as _bacc
    import numpy as _np
    from concourse.bass_utils import run_bass_kernel_spmd as _run

    nc = _bacc.Bacc("TRN2", target_bir_lowering=False, num_devices=1)
    arrays, args = {}, []
    for name in _INS:
        a = _np.ascontiguousarray(inputs[name])
        arrays[f"in_{name}"] = a
        args.append(nc.dram_tensor(f"in_{name}", a.shape, mybir.dt.from_np(a.dtype), kind="ExternalInput").ap())
    shape = inputs["L0_attn_x"].shape
    args.append(nc.dram_tensor("out_0", shape, F32, kind="ExternalOutput").ap())
    transformer_layer(nc, *args)
    r = _run(nc, [arrays], core_ids=[0])
    return r.results[0]["out_0"]
```

```python
from contextlib import ExitStack

import concourse.bass as bass
from concourse import mybir

P = 128
TILES = 4
SEQ = P * TILES
DIM = 256
KT = DIM // P
HEADS = 16
HD = DIM // HEADS
GROUPS = 4
HG = HEADS // GROUPS
GP = HG * HD
STACK = 4 * HD
AUG = 2
UNITS = HG * TILES
ALL = GROUPS * UNITS
RING = 8
ROWS = 3
EXPERTS = 8
TOPK = 2
FF = 512
FT = FF // P
SCALE = HD ** -0.5
EPS = 1e-5
ROW = DIM + 4
C_ID, C_DIFF, C_G1, C_E0 = DIM, DIM + 1, DIM + 2, DIM + 3
COL = 32
FAR = 1 << 20

F32 = mybir.dt.float32
F32R = mybir.dt.float32r
BF16 = mybir.dt.bfloat16
U32 = mybir.dt.uint32
ALU = mybir.AluOpType
ACT = mybir.ActivationFunctionType
AX = mybir.AxisListType

ROUNDS = [
    (0, 1, "x1T0", -2), (0, 3, "x1T1", -2), (0, 5, "peak3", -1), (0, 7, "turn1", -1), (0, 9, "xT0", 1),
    (0, 11, "logit", -2), (0, 13, "xT1", 1), (0, 15, "logitT", -2),
    (1, 3, "qk0", 1), (1, 5, "peak0", 0), (1, 7, "turn2", -1), (1, 11, "qk1", 1), (1, 15, "qk2", 1),
    (2, 1, "place", -2), (2, 3, "qk3", 1), (2, 5, "peak1", 0), (2, 7, "turn3", -1), (2, 11, "oT0", -1), (2, 13, "oT1", -1),
    (2, 15, "proj0", -1),
    (3, 3, "proj1", -1), (3, 5, "peak2", 0), (3, 7, "turn0", 0), (3, 11, "v0", 1), (3, 15, "v1", 1),
]
NAMES = [r[2] for r in ROUNDS]
OFFSET = {r[2]: r[3] for r in ROUNDS}
AT = {(r[0], r[1]): r[2] for r in ROUNDS}


def wait(engine, sem, value):
    if not isinstance(value, int) or value > 0:
        engine.wait_ge(sem, value)


def settle(engine, sem):
    engine.sem_inc(sem, 1)


def wait_emptied(engine, s_free, bank_and_value):
    bank, value = bank_and_value
    wait(engine, s_free[bank], value)


class Iteration:

    def __init__(self, pair, odd, n_seq, filling=False):
        self.filling = filling
        self.pair = pair
        self.b = 2 * pair + odd
        self.odd = odd % 2
        self.known = isinstance(pair, int)
        self.n_seq = n_seq

    def on(self, offset):
        return not self.known or 0 <= self.b + offset < self.n_seq

    def rounds_before(self, b, name):
        total = 0
        for c in range(-1, b + 1):
            for n in NAMES:
                if c == b and n == name:
                    return total
                total += 0 <= c + OFFSET[n] < self.n_seq
        return total

    def number(self, name, shift=0):
        if self.known:
            return self.rounds_before(self.b + shift, name), 0
        return (len(NAMES) * (self.odd + shift - 2) + self.rounds_before(2, NAMES[0]) + NAMES.index(name),
                2 * len(NAMES))

    def full(self, name, shift=0):
        known, per_pair = self.number(name, shift)
        return self.pair * per_pair + (known + 1) if per_pair else known + 1

    def pairs(self, offset):
        return (self.pair + (self.odd + offset) // 2) * 16 + 16

    def bank(self, name):
        return self.number(name)[0] % 2

    def emptied(self, name, shift=0, rounds=0):
        known, per_pair = self.number(name, shift)
        known -= rounds
        value = known // 2 + 1
        return known % 2, (self.pair * (per_pair // 2) + value if per_pair else value)


def iterations(engine, n_seq, body, fills=2):
    for b in (-1, 0, 1):
        body(Iteration(b // 2, b % 2, n_seq, b >= 0))
    for first, end in ((1, fills // 2), (fills // 2, n_seq // 2 - 1)):
        if first < end:
            with engine.Fori(first, end) as pair:
                for odd in (0, 1):
                    body(Iteration(pair, odd, n_seq, end == fills // 2))
    for b in range(n_seq - 2, n_seq + 2):
        body(Iteration(b // 2, b % 2, n_seq))


QUARTERS, BLOCK = P // 32, 32
LOADED = 16 * (QUARTERS + 1)
W_PIECES = 3


class Weights:

    def __init__(self, stacks, probs, w1, w2):
        flat = [stack[:].rearrange("p h n -> p (h n)") for stack in stacks]
        half = FT * DIM
        self.w1_hi, self.w1_lo = [[flat[i + j].rearrange("p (k f) -> p k f", k=KT) for j in range(2)] for i in (0, 2)]
        self.w2_hi, self.w2_lo = [[flat[4 + j][:, i * half:(i + 1) * half].rearrange("p (k d) -> p k d", k=FT)
                                   for j in range(2)] for i in range(2)]
        raw = probs[:].rearrange("p r n -> p (r n)")
        self.raw1 = raw[:, 0:KT * 2 * FF].rearrange("p (k f) -> p k f", k=KT)
        self.raw2 = raw[:, KT * 2 * FF:KT * 2 * FF + half].rearrange("p (k d) -> p k d", k=FT)
        self.w1_rows = w1.rearrange("e (a k i) f -> e a i k f", a=QUARTERS, i=BLOCK)
        self.w2_rows = w2.rearrange("e (k p) d -> e p k d", p=P)

    def load(self, engine, e, s_raw):
        for a in range(QUARTERS):
            engine.dma_start(self.raw1[a * BLOCK:(a + 1) * BLOCK], self.w1_rows[e, a]).then_inc(s_raw, 16)
        engine.dma_start(self.raw2, self.w2_rows[e]).then_inc(s_raw, 16)

    def pieces(self, par):
        return [(self.raw1[:, 0], self.w1_hi[par][:, 0], self.w1_lo[par][:, 0]),
                (self.raw1[:, 1], self.w1_hi[par][:, 1], self.w1_lo[par][:, 1]),
                (self.raw2, self.w2_hi[par], self.w2_lo[par])]


def attention(nc, x, w_qkv, w_proj, b_proj, w_gate, x1_dram, table, stacks, probs, weights):
    n_seq = x.shape[0]
    cap = table.shape[0] // EXPERTS
    per = cap // SEQ
    assert cap % SEQ == 0 and per % 2 == 0 and per <= n_seq - 2

    x_rows = x.rearrange("b (p t) c -> b p (t c)", t=TILES)
    x1_rows = x1_dram.rearrange("(b p t) c -> b p t c", p=P, t=TILES)
    table_rows = table.rearrange("(n p t) c -> n p (t c)", p=P, t=TILES)

    with ExitStack() as ctx:
        def sb(name, shape, dt=F32):
            return ctx.enter_context(nc.sbuf_tensor(name, shape, dt))

        def psum(name, shape):
            return ctx.enter_context(nc.psum_tensor(name, shape, F32))

        def sem(name):
            return ctx.enter_context(nc.semaphore(name))

        ps_rows = [psum(f"ps_rows{i}", [P, SEQ]) for i in range(ROWS)]
        ps_cols = [psum(f"ps_cols{i}", [P, SEQ]) for i in range(2)]
        ps_pv = psum("ps_pv", [P, SEQ])
        ps_round = [psum(f"ps_round{i}", [P, SEQ]) for i in range(2)]

        ident = sb("ident", [P, P])
        before = sb("before", [P, P], BF16)
        ones = sb("ones", [P, P], BF16)
        half = sb("half", [P, TILES])
        number = sb("number", [P, EXPERTS])
        w_in = sb("w_in", [P, KT, 3 * DIM])
        w_qk_hi = sb("w_qk_hi", [P, KT, 4, P], F32R)
        w_qk_lo = sb("w_qk_lo", [P, KT, 4, P], F32R)
        w_v_hi = sb("w_v_hi", [P, KT, DIM], F32R)
        w_v_lo = sb("w_v_lo", [P, KT, DIM], F32R)
        w_out = sb("w_out", [P, KT, DIM])
        bias = sb("bias", [P, DIM])
        gate_rows = sb("gate_rows", [EXPERTS, DIM])
        gate_t = sb("gate_t", [P, KT, COL])
        zero_rows = sb("zero_rows", [2 * UNITS, P])
        blank = sb("blank", [P, TILES, ROW])

        xs = [sb(f"xs{i}", [P, TILES, DIM]) for i in range(2)]
        xb = [sb(f"xb{i}", [P, TILES, DIM]) for i in range(2)]
        x_t_hi = sb("x_t_hi", [P, KT, SEQ], F32R)
        x_t_lo = sb("x_t_lo", [P, KT, SEQ], F32R)
        qk_hi = [sb(f"qk_hi{i}", [P, 4, SEQ], F32R) for i in range(2)]
        qk_lo = [sb(f"qk_lo{i}", [P, 4, SEQ], F32R) for i in range(2)]
        v = [sb(f"v{i}", [P, TILES, HEADS, HD + 1]) for i in range(2)]
        q_stack, k_stack = stacks[:GROUPS], stacks[GROUPS:]
        peak = [sb(f"peak{i}", [P, UNITS]) for i in range(2)]
        peak_parts = [sb(f"peak_parts{i}", [P, 2 * UNITS], F32R) for i in range(2)]
        peak_rows = [sb(f"peak_rows{i}", [2 * UNITS, P]) for i in range(2)]
        pv = sb("pv", [P, SEQ])
        rsum = sb("rsum", [P, UNITS])
        o = sb("o", [P, TILES, DIM])
        o_t = sb("o_t", [P, KT, SEQ])
        y = sb("y", [P, TILES, DIM])
        stats = sb("stats", [P, TILES, 6])
        mv = sb("mv", [P, TILES, 2])
        var_eps = sb("var_eps", [P, TILES])
        rstd = sb("rstd", [P, TILES])
        row = [sb(f"row{i}", [P, TILES, ROW]) for i in range(2)]
        x1_t = sb("x1_t", [P, KT, SEQ])
        logit_t = sb("logit_t", [P, SEQ // 2])
        logit = sb("logit", [P, TILES, EXPERTS])
        top = sb("top", [P, TILES, 8])
        top_i = sb("top_i", [P, TILES, 8], U32)
        chosen = sb("chosen", [P, TOPK, TILES])
        hot = sb("hot", [P, TOPK * TILES, EXPERTS])
        both = sb("both", [P, TILES, EXPERTS])
        count = sb("count", [P, TILES, EXPERTS])
        row_count = sb("row_count", [P, EXPERTS], BF16)
        carry = sb("carry", [P, EXPERTS], BF16)
        pos_all = sb("pos_all", [P, TILES, EXPERTS])
        hot_pos = sb("hot_pos", [P, TOPK * TILES, EXPERTS])
        pos = sb("pos", [P, TOPK * TILES])
        over = sb("over", [P, TOPK * TILES])
        slot_f = sb("slot_f", [P, TOPK * TILES])
        slot = sb("slot", [P, TOPK * TILES], U32)
        lead = sb("lead", [P, TILES])
        e_lead = sb("e_lead", [P, TILES])
        e_sum = sb("e_sum", [P, TILES])
        g0 = sb("g0", [P, TILES])
        token = sb("token", [P, TILES])

        s_const = sem("s_const")
        s_zero = sem("s_zero")
        s_pad = sem("s_pad")
        s_weights = sem("s_weights")
        s_wqk = sem("s_wqk")
        s_blank = sem("s_blank")
        s_gate = sem("s_gate")
        s_fill = sem("s_fill")
        s_x = [sem(f"s_x_{parity}") for parity in ("even", "odd")]
        s_xb = sem("s_xb")
        s_stack = [sem(f"s_stack{g}") for g in range(GROUPS)]
        s_aug = [sem(f"s_aug{g}") for g in range(GROUPS)]
        s_rows = sem("s_rows")
        s_max = sem("s_max")
        s_phi = sem("s_phi")
        s_parts = sem("s_parts")
        s_cols = sem("s_cols")
        s_exp = sem("s_exp")
        s_pv = sem("s_pv")
        s_pvout = sem("s_pvout")
        s_full = sem("s_full")
        s_free = [sem(f"s_free{i}") for i in range(2)]
        s_xhi = sem("s_xhi")
        s_hi = sem("s_hi")
        s_rsum = sem("s_rsum")
        s_bn = sem("s_bn")
        s_pool = sem("s_pool")
        s_x1 = sem("s_x1")
        s_y = sem("s_y")
        s_route = sem("s_route")
        s_lead = sem("s_lead")
        s_slot = sem("s_slot")
        s_scatter = sem("s_scatter")
        s_raw = sem("s_raw_a")
        s_whi, s_wlo = sem("s_whi_a"), sem("s_wlo_a")

        s_waited_sp, s_waited_pool = sem("s_waited_sp"), sem("s_waited_pool")
        s_waited_pe, s_waited_dve = sem("s_waited_pe"), sem("s_waited_dve")

        ROUTE = 28
        COUNTED, LED = 15, 16

        block = ctx.enter_context(nc.Block())

        @block.sync
        def _(sp):
            sp.dma_start(xs[0][:].rearrange("p t c -> p (t c)"), x_rows[0]).then_inc(s_x[0], 16)
            sp.dma_start(w_in[:], w_qkv.rearrange("(k p) n -> p k n", p=P)).then_inc(s_weights, 16)
            sp.dma_start(w_out[:], w_proj.rearrange("(k p) n -> p k n", p=P)).then_inc(s_weights, 16)
            sp.dma_start(gate_rows[:], w_gate).then_inc(s_weights, 16)
            sp.dma_start(bias[:], b_proj.rearrange("(a n) -> a n", a=1).to_broadcast([P, DIM])).then_inc(s_weights, 16)
            sp.dma_start(xs[1][:].rearrange("p t c -> p (t c)"), x_rows[1]).then_inc(s_x[1], 16)
            sp.wait_ge(s_zero, 1)

            def body(it):
                b = it.b
                for s in range(4):
                    g, off = (s + 1) % 4, 0 if s < 3 else 1
                    if it.on(off):
                        wait(sp, s_cols, (b + (off - 1)) * 64 + (UNITS * (g + 1)))
                        settle(sp, s_waited_sp)
                        wait_emptied(sp, s_free, it.emptied("qk3", off - 1))
                        if it.known and b + off == 0:
                            sp.wait_ge(s_pad, 3 * g + 3)
                        par = (it.odd + off) % 2
                        m, part = g // 2, slice(GP * (g % 2), GP * (g % 2) + GP)
                        hi, lo = qk_hi[par], qk_lo[par]
                        for r, (a, c) in enumerate([(hi, hi), (lo, hi), (hi, lo), (lo, lo)]):
                            rows = slice(HD * r, HD * r + HD)
                            sp.dma_start(q_stack[g][rows].bitcast(F32), a[part, m, :].bitcast(F32)).then_inc(s_stack[g], 16)
                            sp.dma_start(k_stack[g][rows].bitcast(F32), c[part, 2 + m, :].bitcast(F32)).then_inc(s_stack[g], 16)
                        sp.dma_start(q_stack[g][STACK:STACK + AUG].bitcast(F32), zero_rows[:]).then_inc(s_stack[g], 16)
                    g, off = (s - 1) % 4, 0 if s > 0 else -1
                    if it.on(off):
                        wait_emptied(sp, s_free, it.emptied(f"peak{g}"))
                        sp.dma_start(q_stack[g][STACK:STACK + AUG].bitcast(F32), peak_rows[g % 2][:]).then_inc(s_aug[g], 16)
                    if s == 0 and it.on(-2):
                        wait(sp, s_x1, (b - 1) * TILES)
                        settle(sp, s_waited_sp)
                        sp.dma_start(x1_rows[b - 2], row[it.odd][:, :, 0:DIM]).then_inc(s_y, 16)
                    if s == 3 and it.on(2) and not (it.known and b < 0):
                        wait(sp, s_xb, b + 1)
                        settle(sp, s_waited_sp)
                        if it.on(0):
                            sp.wait_ge(s_full, it.full("xT1", -1))
                            settle(sp, s_waited_sp)
                        sp.dma_start(xs[it.odd][:].rearrange("p t c -> p (t c)"), x_rows[b + 2]).then_inc(s_x[it.odd], 16)
                    if s == 3 and it.known and b == n_seq:
                        sp.wait_ge(s_pv, n_seq * UNITS)
                        weights.load(sp, 0, s_raw)
                    if it.filling:
                        if it.known:
                            sp.wait_ge(s_blank, 2)
                        for e in (2 * s, 2 * s + 1):
                            sp.dma_start(table_rows[b + e * per],
                                         blank[:].rearrange("p t c -> p (t c)")).then_inc(s_fill, 16)

            iterations(sp, n_seq, body, per)
            sp.wait_ge(s_fill, 16 * EXPERTS * per)
            sp.wait_ge(s_y, 16 * n_seq)

        @block.gpsimd
        def _(pool):
            pool.memset(ident[:], 0.0).then_inc(s_const, 1)
            pool.memset(before[:], 1.0).then_inc(s_const, 1)
            pool.memset(ones[:], 1.0).then_inc(s_const, 1)
            pool.memset(half[:], -0.5).then_inc(s_const, 1)
            pool.memset(blank[:], 0.0).then_inc(s_blank, 1)
            pool.iota(number[:], [[1, EXPERTS]], base=0, channel_multiplier=0,
                      allow_small_or_imprecise_dtypes=True).then_inc(s_const, 1)
            pool.iota(token[:], [[1, TILES]], base=0, channel_multiplier=TILES,
                      allow_small_or_imprecise_dtypes=True).then_inc(s_const, 1)
            pool.wait_ge(s_const, 6)
            pool.affine_select(out=ident[:], in_=ident[:], compare_op=ALU.not_equal, fill=1.0, base=0,
                               pattern=[[-1, P]], channel_multiplier=1).then_inc(s_const, 1)
            pool.affine_select(out=before[:], in_=before[:], compare_op=ALU.is_gt, fill=0.0, base=0,
                               pattern=[[1, P]], channel_multiplier=-1).then_inc(s_const, 1)
            pool.wait_ge(s_blank, 1)
            pool.memset(blank[:].bitcast(U32)[:, :, C_ID:C_ID + 1], FAR).then_inc(s_blank, 1)
            for g in range(GROUPS):
                if g == 0:
                    pool.wait_ge(s_blank, 2)
                else:
                    pool.wait_ge(s_pad, 3 * g)
                pool.memset(k_stack[g][STACK:].bitcast(F32), 0.0).then_inc(s_pad, 1)
                pool.wait_ge(s_pad, 3 * g + 1)
                pool.memset(k_stack[g][STACK:STACK + AUG].bitcast(F32), 1.0).then_inc(s_pad, 1)
                pool.wait_ge(s_pad, 3 * g + 2)
                pool.memset(q_stack[g][STACK:].bitcast(F32), 0.0).then_inc(s_pad, 1)
            pool.wait_ge(s_pad, 3 * GROUPS)
            pool.wait_ge(s_weights, 64)

            def body(it):
                b = it.b
                for s in range(4):
                    if s == 3:
                        if it.on(-1):
                            pool.wait_ge(s_bn, 8 * b)
                            settle(pool, s_waited_pool)
                            pool.tensor_scalar(var_eps[:], mv[:, :, 1], EPS, None, ALU.add).then_inc(s_pool, 1)
                            pool.wait_ge(s_pool, 2 * b - 1)
                            pool.tensor_tensor(rstd[:], var_eps[:], half[:], ALU.pow).then_inc(s_pool, 1)
                            pool.wait_ge(s_pool, 2 * b)
                            wait(pool, s_scatter, (b - 2) * (16 * TOPK * TILES))
                            wait(pool, s_y, (b - 2) * 16)
                            settle(pool, s_waited_pool)
                            for t in range(0 if it.known and b == n_seq else TILES):
                                pool.tensor_scalar(row[1 - it.odd][:, t, 0:DIM], y[:, t, :], mv[:, t, 0:1], rstd[:, t:t + 1],
                                                   ALU.subtract, ALU.mult).then_inc(s_x1, 1)
                        if it.on(1):
                            pool.wait_ge(s_x[1 - it.odd], it.pairs(1))
                            if it.on(-1):
                                wait_emptied(pool, s_free, it.emptied("proj1"))
                            pool.tensor_tensor(xb[(it.odd + 1) % 2][:], xs[1 - it.odd][:],
                                               bias[:].rearrange("p (a c) -> p a c", a=1).to_broadcast([P, TILES, DIM]),
                                               ALU.add).then_inc(s_xb, 1)
                        if it.on(-2):
                            pool.wait_ge(s_slot, b - 1)
                            pool.wait_ge(s_fill, (b - 1) * (16 * EXPERTS) if it.filling else 16 * EXPERTS * per)
                            settle(pool, s_waited_pool)
                            for k in range(TOPK):
                                for t in range(TILES):
                                    c = k * TILES + t
                                    pool.indirect_dma_start(
                                        table, bass.IndirectOffsetOnAxis(ap=slot[:, c:c + 1], axis=0), row[it.odd][:, t, :], None,
                                        bounds_check=table.shape[0] - 1, oob_is_err=False).then_inc(s_scatter, 16)

            iterations(pool, n_seq, body, per)
            pool.wait_ge(s_scatter, 16 * TOPK * TILES * n_seq)

        @block.tensor
        def _(pe):
            pe.wait_ge(s_weights, 64)
            pe.wait_ge(s_const, 8)
            for k in range(KT):
                last = pe.transpose(ps_round[0][:, k * EXPERTS:(k + 1) * EXPERTS], gate_rows[:, k * P:(k + 1) * P],
                                    ident[0:EXPERTS, 0:EXPERTS])
            last.then_inc(s_gate, 1)
            pe.wait_ge(s_gate, 2)
            pe.wait_ge(s_wqk, 2)
            pe.wait_ge(s_zero, 2)

            def round_(it, name):
                b = it.b
                ps_m = ps_round[it.bank(name)]
                wait_emptied(pe, s_free, it.emptied(name, rounds=2))
                kind, n = name.rstrip("0123"), int(name[-1]) if name[-1].isdigit() else 0

                def result_of(earlier, shift=0):
                    if it.emptied(earlier, shift)[0] != it.bank(name):
                        wait_emptied(pe, s_free, it.emptied(earlier, shift))

                if kind == "peak":
                    pe.wait_ge(s_parts, (b + OFFSET[name]) * GROUPS + (n + 1))
                    last = pe.transpose(ps_m[0:2 * UNITS, 0:P], peak_parts[n % 2][:].bitcast(F32), ident[:])
                elif kind == "xT":
                    pe.wait_ge(s_x[1 - it.odd], it.pairs(1))
                    for t in range(TILES):
                        last = pe.transpose(ps_m[:, t * P:(t + 1) * P], xs[1 - it.odd][:, t, n * P:(n + 1) * P], ident[:])
                elif kind == "qk":
                    if n == 0:
                        result_of("xT1")
                    for k in range(KT):
                        for p, (w, tok) in enumerate([(w_qk_hi, x_t_hi), (w_qk_hi, x_t_lo), (w_qk_lo, x_t_hi)]):
                            last = pe.matmul(ps_m[:], w[:, k, n, :], tok[:, k, :], start=k + p == 0,
                                             stop=(k, p) == (KT - 1, 2))
                elif kind == "v":
                    for t in range(2):
                        for k in range(KT):
                            tok = slice((2 * n + t) * P, (2 * n + t + 1) * P)
                            for p, (xt, w) in enumerate([(x_t_hi, w_v_hi), (x_t_hi, w_v_lo), (x_t_lo, w_v_hi)]):
                                last = pe.matmul(ps_m[:, t * DIM:(t + 1) * DIM], xt[:, k, tok], w[:, k, :],
                                                 start=k + p == 0, stop=(k, p) == (KT - 1, 2))
                elif kind == "turn":
                    pe.wait_ge(s_pvout, (b + OFFSET[name]) * GROUPS + (n + 1))
                    for t in range(TILES):
                        last = pe.transpose(ps_m[:, t * P:(t + 1) * P], pv[:, t * P:(t + 1) * P], ident[:])
                elif kind == "oT":
                    if n == 0:
                        result_of("turn3")
                        settle(pe, s_waited_pe)
                    for t in range(TILES):
                        last = pe.transpose(ps_m[:, t * P:(t + 1) * P], o[:, t, n * P:(n + 1) * P], ident[:])
                elif kind == "proj":
                    if n == 0:
                        result_of("oT1")
                    for t in range(2):
                        for k in range(KT):
                            tok = slice((2 * n + t) * P, (2 * n + t + 1) * P)
                            last = pe.matmul(ps_m[:, t * DIM:(t + 1) * DIM], o_t[:, k, tok], w_out[:, k, :],
                                             start=k == 0, stop=k == KT - 1)
                elif kind == "x1T":
                    pe.wait_ge(s_x1, (b - 1) * TILES)
                    for t in range(TILES):
                        last = pe.transpose(ps_m[:, t * P:(t + 1) * P], row[it.odd][:, t, n * P:(n + 1) * P], ident[:])
                elif kind == "logit":
                    result_of("x1T1")
                    for h in range(2):
                        for k in range(KT):
                            c = COL * (KT * h + k)
                            last = pe.matmul(ps_m[c:c + COL, 0:2 * P].rearrange("p (c q) -> p c q", c=2), gate_t[:, k, :],
                                             x1_t[:, k, :].rearrange("p (c h q) -> p h c q", c=2, h=2)[:, h],
                                             start=True, stop=True)
                elif kind == "logitT":
                    result_of("logit")
                    for c in range(2):
                        last = pe.transpose(ps_m[:, c * P:(c + 1) * P], logit_t[:, c * P:(c + 1) * P], ident[:])
                else:
                    pe.wait_ge(s_route, (b - 2) * ROUTE + COUNTED)
                    pe.matmul(ps_m[:, 0:EXPERTS], before[:], row_count[:], start=True, stop=False)
                    last = pe.matmul(ps_m[:, 0:EXPERTS], ones[:], carry[:], start=False, stop=True)
                last.then_inc(s_full, 1)

            def body(it):
                b = it.b
                for s in range(4):
                    for j in range(UNITS):
                        if it.on(0):
                            if j == 0:
                                pe.wait_ge(s_stack[s], (b + 1) * (16 * 9))
                            n = s * UNITS + j
                            last_use = n - ROWS if n >= ROWS else (ALL - 1 - (ALL - 1 - n) % ROWS) - ALL
                            wait(pe, s_max, b * ALL + (last_use + 1))
                            t, h = j % TILES, j // TILES
                            pe.matmul(ps_rows[n % ROWS][:], q_stack[s][:, h, t * P:(t + 1) * P],
                                      k_stack[s][:, h, :], start=True, stop=True).then_inc(s_rows, 1)
                        g, off = (s + 2) % 4, -1 if s < 2 else 0
                        if it.on(off):
                            if j == 0:
                                pe.wait_ge(s_aug[g], (b + (off + 1)) * 16)
                            wait(pe, s_exp, (b + off) * 64 + (16 * g + j - 1))
                            t, h = j // HG, j % HG
                            pe.matmul(ps_cols[j % 2][:], k_stack[g][:, h, t * P:(t + 1) * P], q_stack[g][:, h, :],
                                      start=True, stop=True).then_inc(s_cols, 1)
                        if j % HG == 1:
                            t = j // HG - 1
                            g, off = ((s + 2) % 4, -1 if s < 2 else 0) if t >= 0 else ((s + 1) % 4, -1 if s < 3 else 0)
                            t %= TILES
                            if it.on(off):
                                if t == 0:
                                    wait(pe, s_pvout, (b + off) * GROUPS + g)
                                pe.wait_ge(s_exp, (b + off) * 64 + (16 * g + HG * (t + 1)))
                                par = (it.odd + off) % 2
                                for h in range(HG):
                                    last = pe.matmul(ps_pv[32 * h:32 * h + HD + 1, :], v[par][:, t, HG * g + h, :],
                                                     probs[:, (HG * t + h) % RING, :], start=t == 0, stop=t == TILES - 1)
                                last.then_inc(s_pv, 1)
                        name = AT.get((s, j))
                        if name and it.on(OFFSET[name]):
                            round_(it, name)

            iterations(pe, n_seq, body)

        @block.scalar
        def _(act):
            def body(it):
                b = it.b

                def full(name):
                    act.wait_ge(s_full, it.full(name))

                def copy_out(name, out, in_):
                    full(name)
                    act.copy(out, in_).then_inc(s_free[it.bank(name)], 1)

                def empty(s, j):
                    name = AT.get((s, j))
                    if name and it.on(OFFSET[name]):
                        ps_m = ps_round[it.bank(name)]
                        kind, n = name.rstrip("0123"), int(name[-1]) if name[-1].isdigit() else 0
                        if kind == "peak":
                            beta = b + OFFSET[name]
                            if n >= 2:
                                act.wait_ge(s_aug[n - 2], (beta + 1) * 16)
                            else:
                                wait(act, s_aug[n + 2], beta * 16)
                            copy_out(name, peak_rows[n % 2][:], ps_m[0:2 * UNITS, 0:P])
                        elif kind == "xT":
                            full(name)
                            act.copy(x_t_hi[:, n, :], ps_m[:]).then_inc(s_xhi, 1)
                        elif kind == "qk":
                            full(name)
                            act.copy(qk_hi[(it.odd + 1) % 2][:, n, :], ps_m[:]).then_inc(s_hi, 1)
                        elif kind == "v":
                            copy_out(name, v[(it.odd + 1) % 2][:, 2 * n:2 * n + 2, :, 0:HD],
                                     ps_m[:].rearrange("p (t h d) -> p t h d", t=2, h=HEADS))
                        elif kind == "oT":
                            copy_out(name, o_t[:, n, :], ps_m[:])
                        elif kind == "x1T":
                            copy_out(name, x1_t[:, n, :], ps_m[:])
                        elif kind == "logit":
                            copy_out(name, logit_t[:], ps_m[:, 0:2 * P])

                for s in range(4):
                    for j in range(UNITS):
                        if j == 2:
                            g, off = (s + 1) % 4, -1 if s < 3 else 0
                            if it.on(off):
                                act.wait_ge(s_pv, (b + off) * 16 + (4 * g + 4))
                                before_ = {0: ("turn0", -1), 1: ("turn1", 0), 2: ("turn2", 0), 3: ("turn3", 0)}[s]
                                if not it.known or (it.b + off) * 4 + g > 0:
                                    act.wait_ge(s_full, it.full(*before_))
                                act.copy(pv[:], ps_pv[:]).then_inc(s_pvout, 1)
                        if j:
                            empty(s, j - 1)
                        g, off = (s + 2) % 4, -1 if s < 2 else 0
                        if it.on(off):
                            if j % HG == 0:
                                wait(act, s_pv, (b + off) * 16 + (4 * g + j // HG - 1))
                            act.wait_ge(s_cols, (b + off) * 64 + (16 * g + j + 1))
                            act.activation(probs[:, j % RING, :], ps_cols[j % 2][:], ACT.Exp,
                                           scale=SCALE).then_inc(s_exp, 1)
                        if j == UNITS - 1:
                            empty(s, j)
                        if s == 2 and j == 2 and it.on(-2):
                            act.wait_ge(s_route, (b - 2) * ROUTE + LED)
                            act.activation(e_lead[:], lead[:], ACT.Exp).then_inc(s_lead, 1)

            iterations(act, n_seq, body)
            act.wait_ge(s_raw, LOADED)
            act.wait_ge(s_cols, n_seq * ALL)
            for raw_w, hi, _ in weights.pieces(0):
                act.copy(hi, raw_w).then_inc(s_whi, 1)

        @block.vector
        def _(dve):
            dve.memset(gate_t[:], 0.0)
            dve.memset(zero_rows[:], 0.0).then_inc(s_zero, 1)
            dve.wait_ge(s_weights, 64)
            def split_weights(part):
                for m in range(4):
                    for g in range(2):
                        for k in range(KT):
                            raw = w_in[:, k, m * P + g * GP:m * P + (g + 1) * GP].rearrange("p (h r) -> p r h", h=HG)
                            cols = slice(g * GP, (g + 1) * GP)
                            part(*[w[:, k, m, cols].rearrange("p (r h) -> p r h", h=HG) for w in (w_qk_hi, w_qk_lo)],
                                 raw)
                return part(w_v_hi[:], w_v_lo[:], w_in[:, :, 2 * DIM:])

            split_weights(lambda hi, lo, raw: dve.tensor_copy(hi, raw)).then_inc(s_wqk, 1)
            dve.wait_ge(s_wqk, 1)
            split_weights(lambda hi, lo, raw: dve.tensor_tensor(lo, raw, hi.bitcast(F32),
                                                                ALU.subtract)).then_inc(s_wqk, 1)
            dve.wait_ge(s_gate, 1)
            dve.wait_ge(s_zero, 1)
            dve.tensor_copy(gate_t[:, :, 0:EXPERTS],
                            ps_round[0][:, 0:KT * EXPERTS].rearrange("p (k e) -> p k e", k=KT)).then_inc(s_gate, 1)
            for i in range(2):
                dve.memset(v[i][:, :, :, HD:HD + 1], 1.0)
            dve.memset(ps_pv[:], 0.0)
            dve.memset(carry[:], 0.0)
            dve.memset(count[:, 0, :], 0.0).then_inc(s_zero, 1)

            def body(it):
                b = it.b

                def full(name):
                    dve.wait_ge(s_full, it.full(name))

                def turn_sums(name, g):
                    full(name)
                    ps_m = ps_round[it.bank(name)]
                    parts = ps_m[:].rearrange("p (u d) -> p u d", d=32)
                    dve.reciprocal(rsum[:], parts[:, :, HD]).then_inc(s_rsum, 1)

                def turn(name, g):
                    beta = b + OFFSET[name]
                    ps_m = ps_round[it.bank(name)]
                    dve.wait_ge(s_rsum, beta * GROUPS + (g + 1))
                    dve.tensor_tensor(
                        o[:, :, g * GP:(g + 1) * GP].rearrange("p t (h d) -> p t h d", h=HG),
                        ps_m[:].rearrange("p (t h d) -> p t h d", t=TILES, h=HG)[:, :, :, 0:HD],
                        rsum[:].rearrange("p (t h a) -> p t h a", t=TILES, a=1).to_broadcast([P, TILES, HG, HD]),
                        ALU.mult).then_inc(s_free[it.bank(name)], 1)

                def low_part(n):
                    par = (it.odd + 1) % 2
                    dve.wait_ge(s_hi, (b + 1) * 4 + (n + 1))
                    bank = it.bank(f"qk{n}")
                    dve.tensor_tensor(qk_lo[par][:, n, :], ps_round[bank][:], qk_hi[par][:, n, :].bitcast(F32),
                                      ALU.subtract).then_inc(s_free[bank], 1)

                def low_x(n):
                    dve.wait_ge(s_xhi, (b + 1) * KT + (n + 1))
                    bank = it.bank(f"xT{n}")
                    dve.tensor_tensor(x_t_lo[:, n, :], ps_round[bank][:], x_t_hi[:, n, :].bitcast(F32),
                                      ALU.subtract).then_inc(s_free[bank], 1)

                def project(n):
                    beta = b - 1
                    full(f"proj{n}")
                    bank = it.bank(f"proj{n}")
                    tt = slice(2 * n, 2 * n + 2)
                    if n == 0:
                        wait(dve, s_x1, beta * TILES)
                    dve.tensor_tensor(y[:, tt, :], ps_round[bank][:].rearrange("p (t c) -> p t c", t=2),
                                      xb[(it.odd + 1) % 2][:, tt, :], ALU.add).then_inc(s_free[bank], 1)

                def statistics(n):
                    wait_emptied(dve, s_free, it.emptied(f"proj{n}"))
                    for t in (2 * n, 2 * n + 1):
                        dve.bn_stats(stats[:, t, :], y[:, t, :]).then_inc(s_bn, 1)

                def aggregates(n):
                    dve.wait_ge(s_bn, (b - 1) * 8 + (4 * n + 2))
                    settle(dve, s_waited_dve)
                    for t in (2 * n, 2 * n + 1):
                        dve.bn_aggr(mv[:, t, :], stats[:, t, :]).then_inc(s_bn, 1)

                link_no = [0]

                def linked():
                    dve.wait_ge(s_route, (b - 2) * ROUTE + link_no[0])

                def link(ins):
                    link_no[0] += 1
                    ins.then_inc(s_route, 1)

                def route_top():
                    full("logitT")
                    bank = it.bank("logitT")
                    halves = ps_round[bank][:, 0:2 * P].rearrange("p (t k e) -> p t e k", t=TILES, k=KT)
                    dve.tensor_reduce(logit[:], halves[:, :, 0:EXPERTS, :], AX.X, ALU.add).then_inc(s_free[bank], 1)
                    wait_emptied(dve, s_free, it.emptied("logitT"))
                    settle(dve, s_waited_dve)
                    for t in range(TILES):
                        link(dve.max(top[:, t, :], logit[:, t, :]))

                def route_experts():
                    linked()
                    settle(dve, s_waited_dve)
                    for t in range(TILES):
                        link(dve.max_index(top_i[:, t, :], top[:, t, :], logit[:, t, :]))

                def route_chosen():
                    linked()
                    link(dve.tensor_copy(chosen[:], top_i[:, :, 0:TOPK].rearrange("p t k -> p k t")))

                def route_hot():
                    linked()
                    link(dve.tensor_tensor(
                        hot[:], number[:].rearrange("p (a e) -> p a e", a=1).to_broadcast([P, TOPK * TILES, EXPERTS]),
                        chosen[:].rearrange("p k (t a) -> p (k t) a", a=1).to_broadcast([P, TOPK * TILES, EXPERTS]),
                        ALU.is_equal))

                def route_both():
                    linked()
                    link(dve.tensor_tensor(both[:], hot[:, 0:TILES, :], hot[:, TILES:, :], ALU.add))

                def route_count(t):
                    linked()
                    link(dve.tensor_tensor(count[:, t, :], count[:, t - 1, :], both[:, t - 1, :], ALU.add))

                def route_total():
                    linked()
                    link(dve.tensor_tensor(row_count[:], count[:, TILES - 1, :], both[:, TILES - 1, :], ALU.add))
                    link(dve.tensor_tensor(lead[:], top[:, :, 1], top[:, :, 0], ALU.subtract))

                def route_place():
                    full("place")
                    bank = it.bank("place")
                    base = ps_round[bank][:, 0:EXPERTS].rearrange("p (a e) -> p a e", a=1).to_broadcast([P, TILES, EXPERTS])
                    dve.tensor_tensor(pos_all[:], count[:], base, ALU.add).then_inc(s_free[bank], 1)
                    link(dve.tensor_tensor(carry[:], carry[:], row_count[:], ALU.add))

                def route_own():
                    wait_emptied(dve, s_free, it.emptied("place"))
                    for k in range(TOPK):
                        link(dve.tensor_tensor(hot_pos[:, k * TILES:(k + 1) * TILES, :],
                                               hot[:, k * TILES:(k + 1) * TILES, :], pos_all[:], ALU.mult))

                def route_pos():
                    linked()
                    link(dve.tensor_reduce(pos[:], hot_pos[:], AX.X, ALU.add))

                def route_slots():
                    linked()
                    link(dve.tensor_scalar(over[:], pos[:], float(cap), float(FAR), ALU.is_ge, ALU.mult))
                    link(dve.scalar_tensor_tensor(slot_f[:], chosen[:].rearrange("p k t -> p (k t)"), float(cap),
                                                  pos[:], ALU.mult, ALU.add))

                def route_sum():
                    wait(dve, s_scatter, (b - 2) * (16 * TOPK * TILES))
                    settle(dve, s_waited_dve)
                    linked()
                    link(dve.tensor_tensor(slot[:], slot_f[:], over[:], ALU.add))

                def route_gates(n):
                    if n == 0:
                        dve.wait_ge(s_lead, b - 1)
                        link(dve.tensor_scalar(e_sum[:], e_lead[:], 1.0, None, ALU.add))
                        return
                    linked()
                    if n == 1:
                        link(dve.reciprocal(g0[:], e_sum[:]))
                    elif n == 2:
                        link(dve.tensor_tensor(row[it.odd][:, :, C_G1], e_lead[:], g0[:], ALU.mult))
                    else:
                        link(dve.tensor_tensor(row[it.odd][:, :, C_DIFF], g0[:], row[it.odd][:, :, C_G1], ALU.subtract))
                        dve.tensor_copy(row[it.odd][:, :, C_E0], chosen[:, 0, :])
                        link(dve.tensor_copy(row[it.odd][:].bitcast(U32)[:, :, C_ID], token[:]))
                        linked()
                        dve.tensor_scalar(token[:], token[:], float(SEQ), None, ALU.add).then_inc(s_slot, 1)

                norm = {(3, 0): (project, 0), (3, 3): (statistics, 0), (3, 4): (aggregates, 0),
                        (3, 5): (project, 1), (3, 6): (statistics, 1), (3, 7): (aggregates, 1)}
                route = {(1, 3): (route_top,), (1, 4): (route_experts,), (1, 6): (route_chosen,), (1, 7): (route_hot,),
                         (1, 10): (route_both,), (1, 11): (route_count, 1), (1, 12): (route_count, 2),
                         (1, 14): (route_count, 3), (1, 15): (route_total,), (2, 3): (route_place,),
                         (2, 4): (route_own,), (2, 6): (route_pos,), (2, 7): (route_slots,), (2, 10): (route_sum,),
                         (2, 11): (route_gates, 0), (2, 12): (route_gates, 1), (2, 14): (route_gates, 2),
                         (2, 15): (route_gates, 3)}
                for s in range(4):
                    for j in range(UNITS):
                        if (s, j) in route and it.on(-2):
                            route[s, j][0](*route[s, j][1:])
                        if it.on(0):
                            n = s * UNITS + j
                            dve.wait_ge(s_rows, b * ALL + (n + 1))
                            if j == 0:
                                wait(dve, s_parts, b * GROUPS + (s - 1))
                            dve.tensor_reduce(peak[s % 2][:, j:j + 1], ps_rows[n % ROWS][:], AX.X, ALU.max,
                                              negate=True).then_inc(s_max, 1)
                        g, off = (s - 1) % 4, 0 if s > 0 else -1
                        if j in (1, 2) and it.on(off):
                            parts = peak_parts[g % 2]
                            if j == 1:
                                if not it.known or (b + off, g) >= (0, 2):
                                    dve.wait_ge(s_full, it.full(f"peak{(g - 2) % 4}", -1 if g in (0, 3) else 0))
                                dve.wait_ge(s_max, b * ALL + s * UNITS)
                                dve.tensor_copy(parts[:, 0:UNITS], peak[g % 2][:]).then_inc(s_phi, 1)
                            else:
                                dve.wait_ge(s_phi, b * GROUPS + s)
                                dve.tensor_tensor(parts[:, UNITS:], peak[g % 2][:], parts[:, 0:UNITS].bitcast(F32),
                                                  ALU.subtract).then_inc(s_parts, 1)
                        if j in (8, 9) and it.on(-1 if s < 3 else 0):
                            (turn_sums if j == 8 else turn)(f"turn{(s + 1) % 4}", (s + 1) % 4)
                        low = {(1, 5): 0, (1, 13): 1, (2, 0): 2, (2, 5): 3}
                        if it.on(1) and (s, j) in low:
                            low_part(low[s, j])
                        if it.on(1) and s == 0 and j in (11, 15):
                            low_x((j - 11) // 4)
                        if (s, j) in norm and it.on(-1):
                            norm[s, j][0](norm[s, j][1])
                if it.known and b == n_seq:
                    dve.wait_ge(s_pool, 2 * b)
                    dve.wait_ge(s_scatter, (b - 2) * (16 * TOPK * TILES))
                    dve.wait_ge(s_y, (b - 2) * 16)
                    for t in range(TILES):
                        dve.tensor_scalar(row[1 - it.odd][:, t, 0:DIM], y[:, t, :], mv[:, t, 0:1], rstd[:, t:t + 1],
                                          ALU.subtract, ALU.mult).then_inc(s_x1, 1)

            iterations(dve, n_seq, body)
            for i, (raw_w, hi, lo) in enumerate(weights.pieces(0)):
                dve.wait_ge(s_whi, i + 1)
                dve.tensor_tensor(lo, raw_w, hi.bitcast(F32), ALU.subtract).then_inc(s_wlo, 1)


def experts(nc, table, weights, x1_dram):
    cap = table.shape[0] // EXPERTS
    per = cap // SEQ
    n_chunks = EXPERTS * per
    n_tokens = x1_dram.shape[0]
    assert cap % SEQ == 0 and per % 2 == 0 and EXPERTS % 2 == 0 and EXPERTS > 4 and per > 2
    WIDTH = DIM // QUARTERS
    chunk_x = table[:, 0:DIM].rearrange("(n b j) (a c) -> n a j b c", b=SEQ // BLOCK, j=BLOCK, a=QUARTERS)
    chunk_meta = table[:, DIM:ROW].rearrange("(n t p) c -> n p t c", p=P, t=TILES)

    with ExitStack() as ctx:
        def sb(name, shape, dt=F32):
            return ctx.enter_context(nc.sbuf_tensor(name, shape, dt))

        def psum(name, shape):
            return ctx.enter_context(nc.psum_tensor(name, shape, F32))

        def sem(name):
            return ctx.enter_context(nc.semaphore(name))

        ps_hid = [psum(f"ps_hid{i}", [P, 2, SEQ]) for i in range(2)]
        ps_out = psum("ps_out", [P, TILES, DIM])

        quarters = [sb(f"quarters{i}", [P, SEQ // BLOCK, WIDTH]) for i in range(2)]
        meta_rows = [sb(f"meta_rows{i}", [P, TILES, ROW - DIM]) for i in range(2)]
        turned = sb("turned", [P, KT, SEQ])
        x_hi = [sb(f"x_hi{i}", [P, KT, SEQ], F32R) for i in range(2)]
        x_lo = [sb(f"x_lo{i}", [P, KT, SEQ], F32R) for i in range(2)]
        w1_hi, w1_lo, w2_hi, w2_lo = weights.w1_hi, weights.w1_lo, weights.w2_hi, weights.w2_lo
        act_in = [sb(f"act_in{i}", [P, SEQ]) for i in range(2)]
        hid = [sb(f"hid{i}", [P, SEQ]) for i in range(2)]
        h_hi = [sb(f"h_hi{i}", [P, FT, SEQ], F32R) for i in range(2)]
        h_lo = [sb(f"h_lo{i}", [P, FT, SEQ], F32R) for i in range(2)]
        out = [sb(f"out{i}", [P, TILES, DIM]) for i in range(2)]
        gate = [sb(f"gate{i}", [P, TILES]) for i in range(2)]
        gate_part = sb("gate_part", [P, TILES])
        token = [sb(f"token{i}", [P, TILES], U32) for i in range(2)]
        expert_no = sb("expert_no", [P, 1])

        s_rows = [sem(f"s_rows{i}") for i in range(2)]
        s_raw = sem("s_raw")
        s_whi = sem("s_whi")
        s_w = sem("s_w")
        s_turn = sem("s_turn")
        s_xhi = sem("s_xhi")
        s_xlo = sem("s_xlo")
        s_hid = sem("s_hid")
        s_gelu = sem("s_gelu")
        s_mul = sem("s_mul")
        s_hhi = sem("s_hhi")
        s_hlo = sem("s_hlo")
        s_out = sem("s_out")
        s_gp = sem("s_gp")
        s_meta = sem("s_meta")
        s_scaled = sem("s_scaled")
        s_add = sem("s_add")
        s_eno = sem("s_eno")

        s_waited_sp, s_waited_pool = sem("s_waited_sp_e"), sem("s_waited_pool_e")

        ADDED = 16 * TILES

        class Chunk:

            def __init__(self, e, par, lead, half, odd, last=False):
                self.e, self.par, self.lead, self.half, self.odd, self.last = e, par, lead, half, odd, last
                self.n = half * 2 + odd
                self.first = isinstance(half, int) and self.n == 0
                self.final_expert = isinstance(e, int) and e == EXPERTS - 1

        def chunks(engine, body):
            halves = per // 2

            def expert(e, par, final=False):
                for odd in range(2):
                    body(Chunk(e, par, True, e * halves, odd))
                with engine.Fori(1, halves - 1 if final else halves) as i:
                    for odd in range(2):
                        body(Chunk(e, par, False, e * halves + i, odd))
                if final:
                    for odd in range(2):
                        body(Chunk(e, par, False, e * halves + halves - 1, odd, last=True))

            expert(0, 0)
            expert(1, 1)
            with engine.Fori(1, EXPERTS // 2 - 1) as pair:
                expert(pair * 2, 0)
                expert(pair * 2 + 1, 1)
            expert(EXPERTS - 2, 0)
            expert(EXPERTS - 1, 1, final=True)

        block = ctx.enter_context(nc.Block())

        @block.sync
        def _(sp):
            def load_rows(odd, n):
                for a in range(QUARTERS):
                    sp.dma_start(quarters[odd][a * BLOCK:(a + 1) * BLOCK], chunk_x[n, a]).then_inc(s_rows[odd], 16)
                sp.dma_start(meta_rows[odd][:], chunk_meta[n]).then_inc(s_rows[odd], 16)

            load_rows(0, 0)
            load_rows(1, 1)

            def body(k):
                if k.lead and k.odd and not k.final_expert:
                    wait(sp, s_w, k.e * W_PIECES)
                    settle(sp, s_waited_sp)
                    weights.load(sp, k.e + 1, s_raw)
                if not k.last:
                    sp.wait_ge(s_turn, k.n * KT + KT)
                    settle(sp, s_waited_sp)
                    sp.wait_ge(s_meta, k.n + 1)
                    settle(sp, s_waited_sp)
                    load_rows(k.odd, k.n + 2)

            chunks(sp, body)
            sp.wait_ge(s_add, n_chunks * ADDED)

        @block.gpsimd
        def _(pool):
            def add_out(buf, n):
                pool.wait_ge(s_scaled, n * TILES + TILES)
                wait(pool, s_add, n * ADDED)
                settle(pool, s_waited_pool)
                for t in range(TILES):
                    pool.indirect_dma_start(
                        x1_dram, bass.IndirectOffsetOnAxis(ap=token[buf][:, t:t + 1], axis=0), out[buf][:, t, :], None,
                        bounds_check=n_tokens - 1, oob_is_err=False, compute_op=ALU.add).then_inc(s_add, 16)

            def body(k):
                if not k.first:
                    add_out(1 - k.odd, k.n - 1)
                if k.lead and k.odd and not k.final_expert:
                    pool.wait_ge(s_raw, k.e * LOADED + LOADED)
                    wait(pool, s_out, k.e * per)
                    settle(pool, s_waited_pool)
                    for i, (raw, hi, lo) in enumerate(weights.pieces(1 - k.par)):
                        pool.tensor_copy(hi, raw).then_inc(s_whi, 1)
                        pool.wait_ge(s_whi, k.e * W_PIECES + (i + 1))
                        pool.tensor_tensor(lo, raw, hi.bitcast(F32), ALU.subtract).then_inc(s_w, 1)

            chunks(pool, body)
            add_out((n_chunks - 1) % 2, n_chunks - 1)

        @block.tensor
        def _(pe):
            def hidden(c, f):
                wait(pe, s_mul, c.n * FT + (f - 1))
                for part in range(2):
                    cols = slice(part * FF + f * P, part * FF + (f + 1) * P)
                    i = 0
                    for k in range(KT):
                        for w, xx in ((w1_hi, x_hi), (w1_lo, x_hi), (w1_hi, x_lo)):
                            last = pe.matmul(ps_hid[f % 2][:, part, :], w[c.par][:, k, cols], xx[c.odd][:, k, :],
                                             start=i == 0, stop=i == 3 * KT - 1)
                            i += 1
                last.then_inc(s_hid, 1)

            def output(par, buf, n):
                wait(pe, s_scaled, n * TILES)
                pe.wait_ge(s_hlo, n * FT + FT)
                for t in range(TILES):
                    i = 0
                    for f in range(FT):
                        for hh, w in ((h_hi, w2_hi), (h_hi, w2_lo), (h_lo, w2_hi)):
                            last = pe.matmul(ps_out[:, t, :], hh[buf][:, f, t * P:(t + 1) * P], w[par][:, f, :],
                                             start=i == 0, stop=i == 3 * FT - 1)
                            i += 1
                last.then_inc(s_out, 1)

            def body(k):
                if k.lead and not k.odd:
                    wait(pe, s_w, k.e * W_PIECES)
                pe.wait_ge(s_xlo, k.n * KT + KT)
                hidden(k, 0)
                hidden(k, 1)
                if not k.first:
                    output(1 - k.par if k.lead and not k.odd else k.par, 1 - k.odd, k.n - 1)
                hidden(k, 2)
                hidden(k, 3)

            chunks(pe, body)
            output(1, (n_chunks - 1) % 2, n_chunks - 1)

        @block.scalar
        def _(act):

            def high_x(buf, n):
                for k in range(KT):
                    act.wait_ge(s_turn, n * KT + (k + 1))
                    act.copy(x_hi[buf][:, k, :], turned[:, k, :]).then_inc(s_xhi, 1)

            def gelu(c, f):
                act.wait_ge(s_hid, c.n * FT + (f + 1))
                act.activation(act_in[f % 2][:], ps_hid[f % 2][:, 0, :], ACT.Gelu).then_inc(s_gelu, 1)

            def high_h(c, f):
                if f == 0:
                    wait(act, s_out, c.n - 1)
                act.wait_ge(s_mul, c.n * FT + (f + 1))
                act.copy(h_hi[c.odd][:, f, :], hid[f % 2][:]).then_inc(s_hhi, 1)

            def scale(buf, n):
                act.wait_ge(s_out, n + 1)
                act.wait_ge(s_meta, n + 1)
                wait(act, s_add, n * ADDED - ADDED)
                for t in range(TILES):
                    act.activation(out[buf][:, t, :], ps_out[:, t, :], ACT.Copy,
                                   scale=gate[buf][:, t:t + 1]).then_inc(s_scaled, 1)

            high_x(0, 0)

            def body(k):
                if not (k.last and k.odd):
                    high_x(1 - k.odd, k.n + 1)
                gelu(k, 0)
                gelu(k, 1)
                high_h(k, 0)
                high_h(k, 1)
                if not k.first:
                    scale(1 - k.odd, k.n - 1)
                gelu(k, 2)
                gelu(k, 3)
                high_h(k, 2)
                high_h(k, 3)

            chunks(act, body)
            scale((n_chunks - 1) % 2, n_chunks - 1)

        @block.vector
        def _(dve):
            dve.memset(expert_no[:], -1.0).then_inc(s_eno, 1)

            def turn(buf, n, loads):
                dve.wait_ge(s_rows[buf], loads)
                wait(dve, s_xlo, n * KT)
                for k in range(KT):
                    dve.transpose(turned[:, k, :].rearrange("p (b j) -> p b j", j=BLOCK),
                                  quarters[buf][:, :, k * BLOCK:(k + 1) * BLOCK]).then_inc(s_turn, 1)

            def low_x(buf, n):
                for k in range(KT):
                    dve.wait_ge(s_xhi, n * KT + (k + 1))
                    dve.tensor_tensor(x_lo[buf][:, k, :], turned[:, k, :], x_hi[buf][:, k, :].bitcast(F32),
                                      ALU.subtract).then_inc(s_xlo, 1)

            def product(c, f):
                dve.wait_ge(s_gelu, c.n * FT + (f + 1))
                wait(dve, s_hlo, c.n * FT + (f - 1))
                dve.tensor_tensor(hid[f % 2][:], ps_hid[f % 2][:, 1, :], act_in[f % 2][:],
                                  ALU.mult).then_inc(s_mul, 1)

            def low_h(c, f):
                dve.wait_ge(s_hhi, c.n * FT + (f + 1))
                dve.tensor_tensor(h_lo[c.odd][:, f, :], hid[f % 2][:], h_hi[c.odd][:, f, :].bitcast(F32),
                                  ALU.subtract).then_inc(s_hlo, 1)

            def meta(c):
                if c.lead and not c.odd:
                    dve.wait_ge(s_eno, c.e + 1)
                    dve.tensor_scalar(expert_no[:], expert_no[:], 1.0, None, ALU.add).then_inc(s_eno, 1)
                dve.wait_ge(s_eno, c.e + 2)
                wait(dve, s_scaled, c.n * TILES - TILES)
                wait(dve, s_add, c.n * ADDED - ADDED)
                r = meta_rows[c.odd]
                dve.scalar_tensor_tensor(gate_part[:], r[:, :, C_E0 - DIM], expert_no[:, 0:1], r[:, :, C_DIFF - DIM],
                                         ALU.is_equal, ALU.mult).then_inc(s_gp, 1)
                dve.wait_ge(s_gp, c.n + 1)
                dve.tensor_tensor(gate[c.odd][:], gate_part[:], r[:, :, C_G1 - DIM], ALU.add)
                dve.tensor_copy(token[c.odd][:], r[:].bitcast(U32)[:, :, C_ID - DIM]).then_inc(s_meta, 1)

            turn(0, 0, LOADED)
            low_x(0, 0)

            def body(k):
                if not (k.last and k.odd):
                    turn(1 - k.odd, k.n + 1, (k.half + (k.odd + 1)) * LOADED)
                    low_x(1 - k.odd, k.n + 1)
                product(k, 0)
                product(k, 1)
                low_h(k, 0)
                low_h(k, 1)
                meta(k)
                product(k, 2)
                product(k, 3)
                low_h(k, 2)
                low_h(k, 3)

            chunks(dve, body)


def final_norm(nc, y_dram, out_dram):
    RING_Y = 4
    n_chunks = y_dram.shape[0] // SEQ
    y_rows = y_dram.rearrange("(n p t) c -> n p (t c)", p=P, t=TILES)
    out_rows = out_dram.rearrange("(n p t) c -> n p (t c)", p=P, t=TILES)
    with ExitStack() as ctx:
        def sb(name, shape, dt=F32):
            return ctx.enter_context(nc.sbuf_tensor(name, shape, dt))

        def sem(name):
            return ctx.enter_context(nc.semaphore(name))

        y = [sb(f"fy{i}", [P, TILES, DIM]) for i in range(RING_Y)]
        z = [sb(f"fz{i}", [P, TILES, DIM]) for i in range(RING_Y)]
        stats = [sb(f"fstats{i}", [P, TILES, 6]) for i in range(RING_Y)]
        mv = [sb(f"fmv{i}", [P, TILES, 2]) for i in range(RING_Y)]
        var_eps = [sb(f"fvar{i}", [P, TILES]) for i in range(RING_Y)]
        rstd = [sb(f"frstd{i}", [P, TILES]) for i in range(RING_Y)]
        half = sb("fhalf", [P, TILES])
        s_in = [sem(f"s_in{i}") for i in range(RING_Y)]
        s_store = [sem(f"s_store{i}") for i in range(RING_Y)]
        s_half = sem("s_fhalf")
        s_bn = sem("s_fbn")
        s_eps = sem("s_feps")
        s_rstd = sem("s_frstd")
        s_norm = sem("s_fnorm")

        s_waited_sp, s_waited_act = sem("s_waited_sp_f"), sem("s_waited_act_f")
        s_waited_pool, s_waited_dve = sem("s_waited_pool_f"), sem("s_waited_dve_f")

        def rings(engine, body):
            for r in range(RING_Y):
                body(r, r, 0)
            with engine.Fori(1, n_chunks // RING_Y) as q:
                for r in range(RING_Y):
                    body(q * RING_Y + r, r, q)

        block = ctx.enter_context(nc.Block())

        @block.sync
        def _(sp):
            def body(i, r, q):
                wait(sp, s_norm, i * TILES - (RING_Y - 1) * TILES)
                if not isinstance(i, int):
                    settle(sp, s_waited_sp)
                sp.dma_start(y[r][:].rearrange("p t c -> p (t c)"), y_rows[i]).then_inc(s_in[r], 16)

            rings(sp, body)

        @block.scalar
        def _(act):
            def body(i, r, q):
                act.wait_ge(s_norm, i * TILES + TILES)
                settle(act, s_waited_act)
                act.dma_start(out_rows[i], z[r][:].rearrange("p t c -> p (t c)")).then_inc(s_store[r], 16)

            rings(act, body)
            for r in range(RING_Y):
                act.wait_ge(s_store[r], 16 * (n_chunks // RING_Y))

        @block.gpsimd
        def _(pool):
            pool.memset(half[:], -0.5).then_inc(s_half, 1)
            pool.wait_ge(s_half, 1)

            def body(i, r, q):
                pool.wait_ge(s_bn, i * 8 + 8)
                wait(pool, s_norm, i * TILES - (RING_Y - 1) * TILES)
                settle(pool, s_waited_pool)
                pool.tensor_scalar(var_eps[r][:], mv[r][:, :, 1], EPS, None, ALU.add).then_inc(s_eps, 1)
                pool.wait_ge(s_eps, i + 1)
                pool.tensor_tensor(rstd[r][:], var_eps[r][:], half[:], ALU.pow).then_inc(s_rstd, 1)

            rings(pool, body)

        @block.vector
        def _(dve):
            def statistics(i, r, q):
                dve.wait_ge(s_in[r], q * 16 + 16)
                for t in range(TILES):
                    dve.bn_stats(stats[r][:, t, :], y[r][:, t, :]).then_inc(s_bn, 1)
                for t in range(TILES):
                    dve.wait_ge(s_bn, i * 8 + (t + 1))
                    settle(dve, s_waited_dve)
                    dve.bn_aggr(mv[r][:, t, :], stats[r][:, t, :]).then_inc(s_bn, 1)

            def normalise(i, r, q):
                dve.wait_ge(s_rstd, i + 1)
                wait(dve, s_store[r], q * 16)
                for t in range(TILES):
                    dve.tensor_scalar(z[r][:, t, :], y[r][:, t, :], mv[r][:, t, 0:1], rstd[r][:, t:t + 1],
                                      ALU.subtract, ALU.mult).then_inc(s_norm, 1)

            def body(i, r, q):
                statistics(i, r, q)
                if isinstance(q, int):
                    if r:
                        normalise(i - 1, r - 1, 0)
                elif r:
                    normalise(i - 1, r - 1, q)
                else:
                    normalise(i - 1, RING_Y - 1, q - 1)

            rings(dve, body)
            normalise(n_chunks - 1, RING_Y - 1, n_chunks // RING_Y - 1)


def transformer_layer(nc, x, w_qkv, w_proj, b_proj, w_gate, w1, w2, out):
    n_tokens = x.shape[0] * x.shape[1]
    cap = n_tokens * TOPK * 5 // 4 // EXPERTS
    x1 = nc.dram_tensor("x1", [n_tokens, DIM], F32).ap()
    table = nc.dram_tensor("expert_rows", [EXPERTS * cap, ROW], F32).ap()
    with ExitStack() as ctx:
        stacks = [ctx.enter_context(nc.sbuf_tensor(f"stack{i}", [P, HG, SEQ], F32R)) for i in range(2 * GROUPS)]
        probs = ctx.enter_context(nc.sbuf_tensor("probs", [P, RING, SEQ], F32))
        weights = Weights(stacks, probs, w1, w2)
        attention(nc, x, w_qkv, w_proj, b_proj, w_gate, x1, table, stacks, probs, weights)
        experts(nc, table, weights, x1)
    final_norm(nc, x1, out.rearrange("b s c -> (b s) c"))


_INS = ["L0_attn_x", "L0_attn_w_qkv", "L0_attn_w_proj", "L0_attn_b_proj", "L0_ffn_Wg", "L0_ffn_W1", "L0_ffn_W2"]


def kernel(**inputs):
    import concourse.bacc as _bacc
    import numpy as _np
    from concourse.bass_utils import run_bass_kernel_spmd as _run

    nc = _bacc.Bacc("TRN2", target_bir_lowering=False, num_devices=1)
    arrays, args = {}, []
    for name in _INS:
        a = _np.ascontiguousarray(inputs[name])
        arrays[f"in_{name}"] = a
        args.append(nc.dram_tensor(f"in_{name}", a.shape, mybir.dt.from_np(a.dtype), kind="ExternalInput").ap())
    shape = inputs["L0_attn_x"].shape
    args.append(nc.dram_tensor("out_0", shape, F32, kind="ExternalOutput").ap())
    transformer_layer(nc, *args)
    r = _run(nc, [arrays], core_ids=[0])
    return r.results[0]["out_0"]
```
